# Optimizing a Trainium2 kernel written in Bass

```python
import numpy as np
import jax
import jax.numpy as jnp

def _softmax(x, axis=-1):
    return jax.nn.softmax(x, axis=axis)

def _gelu(x):
    return jax.nn.gelu(x, approximate=True)

def _silu(x):
    return jax.nn.silu(x)

def _sigmoid(x):
    return jax.nn.sigmoid(x)

def _layernorm(x, axis=-1, eps=1e-05):
    m = jnp.mean(x, axis=axis, keepdims=True)
    v = jnp.var(x, axis=axis, keepdims=True)
    return (x - m) / jnp.sqrt(v + eps)

def _scatter_add(tgt, idx, src, axis=0):
    return tgt.at[idx].add(src)

def _segment_sum(src, seg, n):
    return jax.ops.segment_sum(src, seg, n)
kernel_name = 'mk_adaln_d2_jaxref_r8_6c7550'

def setup_inputs(seed: int=0):
    np.random.seed(seed)
    _w = jnp.asarray

    def _L0_attn_setup():
        import jax, jax.numpy as jnp
        import numpy as np

        def _ssm_forward(x, A_log, B, C, D):
            Bsz, L, M = x.shape
            t = jnp.arange(L, dtype=x.dtype)
            sign = jnp.where(jnp.arange(L) % 2 == 0, 1.0, -1.0).astype(x.dtype)
            P = jnp.exp(t[:, None, None] * A_log[None, :, :])
            W = C.T * B
            K = jnp.einsum('lsm,sm->lm', P, W) * sign[:, None]
            w = jnp.flip(K, axis=0).T[:, None, :]
            xc = jnp.transpose(x, (0, 2, 1))
            y = jax.lax.conv_general_dilated(xc, w, window_strides=(1,), padding=[(L - 1, 0)], dimension_numbers=('NCH', 'OIH', 'NCH'), feature_group_count=M)
            y = jnp.transpose(y, (0, 2, 1))
            return y + x * D[None, None, :]
        D_MODEL, D_STATE, L, BATCH = (128, 16, 512, 2)
        key = jax.random.key(seed)
        k0, k1, k2, k3 = jax.random.split(key, 4)
        x = jax.random.normal(k0, (BATCH, L, D_MODEL), dtype=jnp.float32)
        A_log = jax.random.uniform(k1, (D_STATE, D_MODEL), dtype=jnp.float32, minval=-3.0, maxval=-1.0)
        B = jax.random.normal(k2, (D_STATE, D_MODEL), dtype=jnp.float32) * 0.1
        C = jax.random.normal(k3, (D_MODEL, D_STATE), dtype=jnp.float32) * 0.1
        D = jnp.ones((D_MODEL,), dtype=jnp.float32)
        return {'x': x, 'A_log': A_log, 'B': B, 'C': C, 'D': D}
    _L0_attn_in = _L0_attn_setup()

    def _L0_ffn_setup():
        import jax, jax.numpy as jnp
        import numpy as np
        DIM = 128
        DEPTH = 2
        HEADS = 8
        DIM_HEAD = 64
        WINDOW = 64
        INNER = HEADS * DIM_HEAD
        HID = int(DIM * 4 * 2 / 3)
        B, N = (2, 1024)
        QK_SCALE = 8.0

        def shift_token(t):
            t1, t2 = jnp.split(t, 2, axis=-1)
            t2 = jnp.pad(t2, ((0, 0), (1, 0), (0, 0)))[:, :-1]
            return jnp.concatenate([t1, t2], axis=-1)

        def l2norm(t):
            return t / jnp.clip(jnp.linalg.norm(t, axis=-1, keepdims=True), 1e-12)

        def rotate_half(x):
            x1, x2 = jnp.split(x, 2, axis=-1)
            return jnp.concatenate([-x2, x1], axis=-1)

        def rotary_xpos(q, k):
            n = q.shape[-2]
            half_idx = jnp.arange(0, DIM_HEAD, 2, dtype=jnp.float32)
            inv_freq = 1.0 / 10000.0 ** (half_idx / DIM_HEAD)
            t = jnp.arange(n, dtype=jnp.float32)
            freqs = t[:, None] * inv_freq[None, :]
            freqs = jnp.concatenate([freqs, freqs], axis=-1)
            base = (half_idx + 0.4 * DIM_HEAD) / (1.4 * DIM_HEAD)
            power = (t - n // 2) / float(WINDOW // 2)
            scale = base[None, :] ** power[:, None]
            scale = jnp.concatenate([scale, scale], axis=-1)
            cos, sin = (jnp.cos(freqs), jnp.sin(freqs))
            q = q * cos * scale + rotate_half(q) * sin * scale
            k = k * cos / scale + rotate_half(k) * sin / scale
            return (q, k)

        def local_attention(q, k, v):
            b, h, n, d = q.shape
            w = n // WINDOW
            bq = q.reshape(b, h, w, WINDOW, d) * QK_SCALE
            bk = k.reshape(b, h, w, WINDOW, d)
            bv = v.reshape(b, h, w, WINDOW, d)

            def look_around(t):
                p = jnp.pad(t, ((0, 0), (0, 0), (1, 0), (0, 0), (0, 0)))
                return jnp.concatenate([p[:, :, :w], p[:, :, 1:]], axis=3)
            bk, bv = (look_around(bk), look_around(bv))
            bt = jnp.arange(n).reshape(w, WINDOW)
            btp = jnp.pad(bt, ((1, 0), (0, 0)), constant_values=-1)
            btk = jnp.concatenate([btp[:w], btp[1:]], axis=1)
            sim = jnp.einsum('bhwid,bhwjd->bhwij', bq, bk)
            i = bt[:, :, None]
            j = btk[:, None, :]
            mask = (i < j) | (i > j + WINDOW) | (j == -1)
            sim = jnp.where(mask, -jnp.finfo(sim.dtype).max, sim)
            attn = jax.nn.softmax(sim, axis=-1)
            out = jnp.einsum('bhwij,bhwjd->bhwid', attn, bv)
            return out.reshape(b, h, n, d)

        def _layer(x, wqkv, qs, ksc, wo, lg, lb, w1, b1, w2, b2):
            b, n, _ = x.shape
            h = shift_token(x)
            qkv = h @ wqkv
            q, k, v = jnp.split(qkv, 3, axis=-1)
            to_heads = lambda t: t.reshape(b, n, HEADS, DIM_HEAD).transpose(0, 2, 1, 3)
            q, k, v = (to_heads(q), to_heads(k), to_heads(v))
            q = l2norm(q) * qs
            k = l2norm(k) * ksc
            q, k = rotary_xpos(q, k)
            o = local_attention(q, k, v)
            o = o.transpose(0, 2, 1, 3).reshape(b, n, INNER)
            x = x + o @ wo
            h = shift_token(x)
            mu = h.mean(-1, keepdims=True)
            var = h.var(-1, keepdims=True)
            h = (h - mu) / jnp.sqrt(var + 1e-05) * lg + lb
            h = h @ w1 + b1
            a, g = jnp.split(h, 2, axis=-1)
            h = a * jax.nn.gelu(g, approximate=False)
            x = x + h @ w2 + b2
            return x
        key = jax.random.key(seed)
        ks = jax.random.split(key, 6)
        return {'x': jax.random.normal(ks[0], (B, N, DIM), jnp.float32), 'wqkv': jax.random.normal(ks[1], (DEPTH, DIM, 3 * INNER), jnp.float32) * 0.02, 'q_scale': jnp.ones((DEPTH, DIM_HEAD), jnp.float32), 'k_scale': jnp.ones((DEPTH, DIM_HEAD), jnp.float32), 'wo': jax.random.normal(ks[2], (DEPTH, INNER, DIM), jnp.float32) * 0.02, 'ln_g': jnp.ones((DEPTH, DIM), jnp.float32), 'ln_b': jnp.zeros((DEPTH, DIM), jnp.float32), 'w1': jax.random.normal(ks[3], (DEPTH, DIM, 2 * HID), jnp.float32) * 0.02, 'b1': jnp.zeros((DEPTH, 2 * HID), jnp.float32), 'w2': jax.random.normal(ks[4], (DEPTH, HID, DIM), jnp.float32) * 0.02, 'b2': jnp.zeros((DEPTH, DIM), jnp.float32)}
    _L0_ffn_in = _L0_ffn_setup()
    _L0_c = _w((lambda *s: np.random.randn(*s).astype(np.float32) * 0.05)(4, 128))
    _L0_wmod = _w((lambda *s: np.random.randn(*s).astype(np.float32) * 0.05)(128, 6 * 128) * 128 ** (-0.5))

    def _L1_attn_setup():
        import jax, jax.numpy as jnp
        import numpy as np
        DIMS = 128
        HEADS = 16
        HEAD_DIM = DIMS // HEADS
        key = jax.random.key(seed)
        k_x, k_q, k_k, k_v = jax.random.split(key, 4)
        scale = 1.0 / np.sqrt(DIMS)
        return {'input_seq_embs': jax.random.normal(k_x, (4, 512, DIMS), dtype=jnp.float32), 'W_Q': jax.random.normal(k_q, (DIMS, DIMS), dtype=jnp.float32) * scale, 'W_K': jax.random.normal(k_k, (DIMS, DIMS), dtype=jnp.float32) * scale, 'W_V': jax.random.normal(k_v, (DIMS, DIMS), dtype=jnp.float32) * scale}
    _L1_attn_in = _L1_attn_setup()

    def _L1_ffn_setup():
        import jax, jax.numpy as jnp
        import numpy as np
        D_MODEL = 128
        EXPANSION = 4
        D_HIDDEN = D_MODEL * EXPANSION
        NUM_STAGES = int(np.log2(D_HIDDEN))

        def butterfly(y, weights, dim):
            lead = y.shape[:-1]
            for stage in range(weights.shape[0]):
                s = 2 ** stage
                nb = dim // (2 * s)
                yr = y.reshape(*lead, nb, 2, s)
                a = yr[..., 0, :]
                b = yr[..., 1, :]
                w = weights[stage].reshape(nb, s, 2, 2)
                na = w[..., 0, 0] * a + w[..., 0, 1] * b
                nb2 = w[..., 1, 0] * a + w[..., 1, 1] * b
                y = jnp.stack([na, nb2], axis=-2).reshape(*lead, dim)
            return y
        key = jax.random.key(seed)
        ks = jax.random.split(key, 6)
        B, S = (4, 256)
        x = jax.random.normal(ks[0], (B, S, D_MODEL), jnp.float32)
        W_exp = jax.random.normal(ks[1], (D_MODEL, D_HIDDEN), jnp.float32) * 0.02
        b_exp = jnp.zeros((D_HIDDEN,), jnp.float32)
        up_weights = jax.random.normal(ks[2], (NUM_STAGES, D_HIDDEN // 2, 2, 2), jnp.float32) * 0.02
        up_bias = jnp.zeros((D_HIDDEN,), jnp.float32)
        down_weights = jax.random.normal(ks[3], (NUM_STAGES, D_HIDDEN // 2, 2, 2), jnp.float32) * 0.02
        W_con = jax.random.normal(ks[4], (D_HIDDEN, D_MODEL), jnp.float32) * 0.02
        b_con = jnp.zeros((D_MODEL,), jnp.float32)
        down_bias = jnp.zeros((D_MODEL,), jnp.float32)
        return dict(x=x, W_exp=W_exp, b_exp=b_exp, up_weights=up_weights, up_bias=up_bias, down_weights=down_weights, W_con=W_con, b_con=b_con, down_bias=down_bias)
    _L1_ffn_in = _L1_ffn_setup()
    _L1_c = _w((lambda *s: np.random.randn(*s).astype(np.float32) * 0.05)(4, 128))
    _L1_wmod = _w((lambda *s: np.random.randn(*s).astype(np.float32) * 0.05)(128, 6 * 128) * 128 ** (-0.5))
    _d = {'L0_attn_x': _L0_attn_in['x'], 'L0_attn_A_log': _L0_attn_in['A_log'], 'L0_attn_B': _L0_attn_in['B'], 'L0_attn_C': _L0_attn_in['C'], 'L0_attn_D': _L0_attn_in['D'], 'L0_ffn_wqkv': _L0_ffn_in['wqkv'], 'L0_ffn_q_scale': _L0_ffn_in['q_scale'], 'L0_ffn_k_scale': _L0_ffn_in['k_scale'], 'L0_ffn_wo': _L0_ffn_in['wo'], 'L0_ffn_ln_g': _L0_ffn_in['ln_g'], 'L0_ffn_ln_b': _L0_ffn_in['ln_b'], 'L0_ffn_w1': _L0_ffn_in['w1'], 'L0_ffn_b1': _L0_ffn_in['b1'], 'L0_ffn_w2': _L0_ffn_in['w2'], 'L0_ffn_b2': _L0_ffn_in['b2'], 'L0_c': _L0_c, 'L0_wmod': _L0_wmod, 'L1_attn_W_Q': _L1_attn_in['W_Q'], 'L1_attn_W_K': _L1_attn_in['W_K'], 'L1_attn_W_V': _L1_attn_in['W_V'], 'L1_ffn_W_exp': _L1_ffn_in['W_exp'], 'L1_ffn_b_exp': _L1_ffn_in['b_exp'], 'L1_ffn_up_weights': _L1_ffn_in['up_weights'], 'L1_ffn_up_bias': _L1_ffn_in['up_bias'], 'L1_ffn_down_weights': _L1_ffn_in['down_weights'], 'L1_ffn_W_con': _L1_ffn_in['W_con'], 'L1_ffn_b_con': _L1_ffn_in['b_con'], 'L1_ffn_down_bias': _L1_ffn_in['down_bias'], 'L1_c': _L1_c, 'L1_wmod': _L1_wmod}
    _x0 = _d['L0_attn_x']
    _d['L0_attn_x'] = jax.random.normal(jax.random.fold_in(jax.random.key(seed), 1), (4, 1024, 128), dtype=_x0.dtype)
    del _x0
    return _d

def reference(L0_attn_x, L0_attn_A_log, L0_attn_B, L0_attn_C, L0_attn_D, L0_ffn_wqkv, L0_ffn_q_scale, L0_ffn_k_scale, L0_ffn_wo, L0_ffn_ln_g, L0_ffn_ln_b, L0_ffn_w1, L0_ffn_b1, L0_ffn_w2, L0_ffn_b2, L0_c, L0_wmod, L1_attn_W_Q, L1_attn_W_K, L1_attn_W_V, L1_ffn_W_exp, L1_ffn_b_exp, L1_ffn_up_weights, L1_ffn_up_bias, L1_ffn_down_weights, L1_ffn_W_con, L1_ffn_b_con, L1_ffn_down_bias, L1_c, L1_wmod):

    def _L0_attn_ref(x, A_log, B, C, D):
        import jax, jax.numpy as jnp
        import numpy as np

        def _ssm_forward(x, A_log, B, C, D):
            Bsz, L, M = x.shape
            t = jnp.arange(L, dtype=x.dtype)
            sign = jnp.where(jnp.arange(L) % 2 == 0, 1.0, -1.0).astype(x.dtype)
            P = jnp.exp(t[:, None, None] * A_log[None, :, :])
            W = C.T * B
            K = jnp.einsum('lsm,sm->lm', P, W) * sign[:, None]
            w = jnp.flip(K, axis=0).T[:, None, :]
            xc = jnp.transpose(x, (0, 2, 1))
            y = jax.lax.conv_general_dilated(xc, w, window_strides=(1,), padding=[(L - 1, 0)], dimension_numbers=('NCH', 'OIH', 'NCH'), feature_group_count=M)
            y = jnp.transpose(y, (0, 2, 1))
            return y + x * D[None, None, :]
        return _ssm_forward(x, A_log, B, C, D)

    def _L0_ffn_ref(x, wqkv, q_scale, k_scale, wo, ln_g, ln_b, w1, b1, w2, b2):
        import jax, jax.numpy as jnp
        import numpy as np
        DIM = 128
        DEPTH = 2
        HEADS = 8
        DIM_HEAD = 64
        WINDOW = 64
        INNER = HEADS * DIM_HEAD
        HID = int(DIM * 4 * 2 / 3)
        B, N = (2, 1024)
        QK_SCALE = 8.0

        def shift_token(t):
            t1, t2 = jnp.split(t, 2, axis=-1)
            t2 = jnp.pad(t2, ((0, 0), (1, 0), (0, 0)))[:, :-1]
            return jnp.concatenate([t1, t2], axis=-1)

        def l2norm(t):
            return t / jnp.clip(jnp.linalg.norm(t, axis=-1, keepdims=True), 1e-12)

        def rotate_half(x):
            x1, x2 = jnp.split(x, 2, axis=-1)
            return jnp.concatenate([-x2, x1], axis=-1)

        def rotary_xpos(q, k):
            n = q.shape[-2]
            half_idx = jnp.arange(0, DIM_HEAD, 2, dtype=jnp.float32)
            inv_freq = 1.0 / 10000.0 ** (half_idx / DIM_HEAD)
            t = jnp.arange(n, dtype=jnp.float32)
            freqs = t[:, None] * inv_freq[None, :]
            freqs = jnp.concatenate([freqs, freqs], axis=-1)
            base = (half_idx + 0.4 * DIM_HEAD) / (1.4 * DIM_HEAD)
            power = (t - n // 2) / float(WINDOW // 2)
            scale = base[None, :] ** power[:, None]
            scale = jnp.concatenate([scale, scale], axis=-1)
            cos, sin = (jnp.cos(freqs), jnp.sin(freqs))
            q = q * cos * scale + rotate_half(q) * sin * scale
            k = k * cos / scale + rotate_half(k) * sin / scale
            return (q, k)

        def local_attention(q, k, v):
            b, h, n, d = q.shape
            w = n // WINDOW
            bq = q.reshape(b, h, w, WINDOW, d) * QK_SCALE
            bk = k.reshape(b, h, w, WINDOW, d)
            bv = v.reshape(b, h, w, WINDOW, d)

            def look_around(t):
                p = jnp.pad(t, ((0, 0), (0, 0), (1, 0), (0, 0), (0, 0)))
                return jnp.concatenate([p[:, :, :w], p[:, :, 1:]], axis=3)
            bk, bv = (look_around(bk), look_around(bv))
            bt = jnp.arange(n).reshape(w, WINDOW)
            btp = jnp.pad(bt, ((1, 0), (0, 0)), constant_values=-1)
            btk = jnp.concatenate([btp[:w], btp[1:]], axis=1)
            sim = jnp.einsum('bhwid,bhwjd->bhwij', bq, bk)
            i = bt[:, :, None]
            j = btk[:, None, :]
            mask = (i < j) | (i > j + WINDOW) | (j == -1)
            sim = jnp.where(mask, -jnp.finfo(sim.dtype).max, sim)
            attn = jax.nn.softmax(sim, axis=-1)
            out = jnp.einsum('bhwij,bhwjd->bhwid', attn, bv)
            return out.reshape(b, h, n, d)

        def _layer(x, wqkv, qs, ksc, wo, lg, lb, w1, b1, w2, b2):
            b, n, _ = x.shape
            h = shift_token(x)
            qkv = h @ wqkv
            q, k, v = jnp.split(qkv, 3, axis=-1)
            to_heads = lambda t: t.reshape(b, n, HEADS, DIM_HEAD).transpose(0, 2, 1, 3)
            q, k, v = (to_heads(q), to_heads(k), to_heads(v))
            q = l2norm(q) * qs
            k = l2norm(k) * ksc
            q, k = rotary_xpos(q, k)
            o = local_attention(q, k, v)
            o = o.transpose(0, 2, 1, 3).reshape(b, n, INNER)
            x = x + o @ wo
            h = shift_token(x)
            mu = h.mean(-1, keepdims=True)
            var = h.var(-1, keepdims=True)
            h = (h - mu) / jnp.sqrt(var + 1e-05) * lg + lb
            h = h @ w1 + b1
            a, g = jnp.split(h, 2, axis=-1)
            h = a * jax.nn.gelu(g, approximate=False)
            x = x + h @ w2 + b2
            return x
        for l in range(DEPTH):
            x = _layer(x, wqkv[l], q_scale[l], k_scale[l], wo[l], ln_g[l], ln_b[l], w1[l], b1[l], w2[l], b2[l])
        return x

    def _L1_attn_ref(input_seq_embs, W_Q, W_K, W_V):
        import jax, jax.numpy as jnp
        import numpy as np
        DIMS = 128
        HEADS = 16
        HEAD_DIM = DIMS // HEADS
        B, L, d = input_seq_embs.shape
        H, hd = (HEADS, HEAD_DIM)
        Q = (input_seq_embs @ W_Q.T).reshape(B, L, H, hd)
        K = (input_seq_embs @ W_K.T).reshape(B, L, H, hd)
        V = (input_seq_embs @ W_V.T).reshape(B, L, H, hd)
        sK = jax.nn.softmax(jnp.swapaxes(K, -1, -2), axis=-1)
        tran_V = jnp.einsum('bldh,blhe->blde', sK, V)
        out = jnp.einsum('blhd,blde->blhe', jax.nn.softmax(Q, axis=-1), tran_V)
        return out.reshape(B, L, d)

    def _L1_ffn_ref(x, W_exp, b_exp, up_weights, up_bias, down_weights, W_con, b_con, down_bias):
        import jax, jax.numpy as jnp
        import numpy as np
        D_MODEL = 128
        EXPANSION = 4
        D_HIDDEN = D_MODEL * EXPANSION
        NUM_STAGES = int(np.log2(D_HIDDEN))

        def butterfly(y, weights, dim):
            lead = y.shape[:-1]
            for stage in range(weights.shape[0]):
                s = 2 ** stage
                nb = dim // (2 * s)
                yr = y.reshape(*lead, nb, 2, s)
                a = yr[..., 0, :]
                b = yr[..., 1, :]
                w = weights[stage].reshape(nb, s, 2, 2)
                na = w[..., 0, 0] * a + w[..., 0, 1] * b
                nb2 = w[..., 1, 0] * a + w[..., 1, 1] * b
                y = jnp.stack([na, nb2], axis=-2).reshape(*lead, dim)
            return y
        h = jnp.einsum('bsd,dh->bsh', x, W_exp) + b_exp
        h = butterfly(h, up_weights, D_HIDDEN)
        h = jax.nn.gelu(h + up_bias, approximate=False)
        h = butterfly(h, down_weights, D_HIDDEN)
        y = jnp.einsum('bsh,hd->bsd', h, W_con) + b_con
        return y + down_bias
    x = L0_attn_x
    mod = (_silu(L0_c) @ L0_wmod).reshape(L0_c.shape[0], 6, 1, -1)
    sa, ca, ga, sb, cb, gb = (mod[:, 0], mod[:, 1], mod[:, 2], mod[:, 3], mod[:, 4], mod[:, 5])
    ga = (2 * (ga >= 0) - 1) * jnp.maximum(jnp.abs(ga), 0.25)
    gb = (2 * (gb >= 0) - 1) * jnp.maximum(jnp.abs(gb), 0.25)
    h = _layernorm(x, axis=-1) * (1 + ca) + sa
    x = x + ga * _L0_attn_ref(h, L0_attn_A_log, L0_attn_B, L0_attn_C, L0_attn_D)
    h = _layernorm(x, axis=-1) * (1 + cb) + sb
    x = x + gb * _L0_ffn_ref(h, L0_ffn_wqkv, L0_ffn_q_scale, L0_ffn_k_scale, L0_ffn_wo, L0_ffn_ln_g, L0_ffn_ln_b, L0_ffn_w1, L0_ffn_b1, L0_ffn_w2, L0_ffn_b2)
    mod = (_silu(L1_c) @ L1_wmod).reshape(L1_c.shape[0], 6, 1, -1)
    sa, ca, ga, sb, cb, gb = (mod[:, 0], mod[:, 1], mod[:, 2], mod[:, 3], mod[:, 4], mod[:, 5])
    ga = (2 * (ga >= 0) - 1) * jnp.maximum(jnp.abs(ga), 0.25)
    gb = (2 * (gb >= 0) - 1) * jnp.maximum(jnp.abs(gb), 0.25)
    h = _layernorm(x, axis=-1) * (1 + ca) + sa
    x = x + ga * _L1_attn_ref(h, L1_attn_W_Q, L1_attn_W_K, L1_attn_W_V)
    h = _layernorm(x, axis=-1) * (1 + cb) + sb
    x = x + gb * _L1_ffn_ref(h, L1_ffn_W_exp, L1_ffn_b_exp, L1_ffn_up_weights, L1_ffn_up_bias, L1_ffn_down_weights, L1_ffn_W_con, L1_ffn_b_con, L1_ffn_down_bias)
    return x

_drawn_inputs = setup_inputs


def setup_inputs(seed=0):
    import zlib

    import numpy as np

    out = dict(_drawn_inputs(seed))
    spreads = {'L0_attn_D': (1.0, 0.2),
     'L0_ffn_q_scale': (1.0, 0.6),
     'L0_ffn_k_scale': (1.0, 0.6),
     'L0_ffn_ln_g': (1.0, 0.6),
     'L0_ffn_ln_b': (0.0, 0.8),
     'L0_ffn_b1': (0.0, 0.8),
     'L0_ffn_b2': (0.0, 0.743),
     'L1_ffn_b_exp': (0.0, 0.1),
     'L1_ffn_up_bias': (0.0, 0.1),
     'L1_ffn_b_con': (0.0, 2.0),
     'L1_ffn_down_bias': (0.0, 2.0)}
    factors = {'L0_attn_A_log': 64.0,
     'L0_attn_B': 5.571,
     'L0_attn_C': 5.728,
     'L0_ffn_wqkv': 8.0,
     'L0_ffn_wo': 8.0,
     'L0_ffn_w1': 8.0,
     'L0_ffn_w2': 8.0,
     'L1_attn_W_Q': 8.0,
     'L1_attn_W_K': 8.0,
     'L1_attn_W_V': 8.0,
     'L1_c': 7.323,
     'L1_wmod': 7.342}
    for name, (base, spread) in spreads.items():
        noise = np.random.default_rng([zlib.crc32(name.encode()), seed]).standard_normal(out[name].shape)
        drawn = base * np.exp(spread * noise) if base else spread * noise
        out[name] = jnp.asarray(drawn.astype(out[name].dtype))
    for name, factor in factors.items():
        out[name] = (out[name] * factor).astype(out[name].dtype)
    return out
```

```python
from contextlib import ExitStack
from collections import namedtuple

import numpy as np
import concourse.bass as bass
from concourse import mybir

F32 = mybir.dt.float32
BF16 = mybir.dt.bfloat16
ALU = mybir.AluOpType
ACT = mybir.ActivationFunctionType
AX_X = mybir.AxisListType.X

P = 128
B, N, D = 4, 1024, 128
TOK = B * N
BANK = 512
EPS = 1e-5
ARENA = 25400
LN2 = float(np.log(2.0))

CH = 16
S = 16
CG = P // CH
G = D // CG
NCH = N // CH

DEPTH, HEADS, DH, WIN = 2, 8, 64, 64
INNER = HEADS * DH
PAIRS = HEADS // 2
TILES = TOK // P
TPB = N // P
HID = int(D * 4 * 2 / 3)
HT = [(j, min(P, HID - j)) for j in range(0, HID, P)]
PADN = N + 1
QK_SCALE = 8.0
SS_SCALE = 65536.0

HD1 = 8
HIDDEN = 512
STAGES = 9
GROUPS = TOK // BANK


def shape_constants():
    p = np.arange(P)
    half = np.arange(0, DH, 2, dtype=np.float32)
    inv = (np.float32(1.0) / np.float32(10000.0) ** (half / np.float32(DH))).astype(np.float32)
    t = np.arange(N, dtype=np.float32)
    fr = t[:, None] * inv[None, :]
    fr = np.concatenate([fr, fr], -1).astype(np.float64)
    base = (half + np.float32(0.4 * DH)) / np.float32(1.4 * DH)
    power = (t - N // 2) / np.float32(WIN // 2)
    sc = base[None, :].astype(np.float64) ** power[:, None].astype(np.float64)
    sc = np.concatenate([sc, sc], -1)
    cos, sin = np.cos(fr), np.sin(fr)
    sgn = np.where(np.arange(DH) < DH // 2, 1.0, -1.0)[None, :]
    rope = np.stack([cos * sc * QK_SCALE, cos / sc, sgn * sin * sc * QK_SCALE, sgn * sin / sc], 1)
    rope = rope * SS_SCALE ** 0.5
    rope = rope.reshape(TPB, P, 4 * DH).transpose(1, 0, 2)
    i = (p % WIN)[:, None]
    c = np.arange(WIN)[None, :]
    own = np.where(c <= i, 0.0, -1e38)
    before = np.where(c >= i, 0.0, -1e38)
    first = np.concatenate([own, np.full((P, WIN), -1e38)], 1)
    even = np.concatenate([own, before], 1)
    odd = np.concatenate([before, own], 1)
    masks = np.stack([first] + [even] * (TPB - 1) + [odd], 1)
    chan = p[:, None] // CH == np.arange(CG)[None, :]
    srow = np.zeros((P, P))
    srow[:S] = np.arange(S)[:, None] == p[None, :] % S
    powers = np.tile(np.arange(CH, -1, -1)[None, :], (P, 1))
    signs = np.where(powers % 2 == 0, 1.0, -1.0)
    shift = np.zeros((P, P + CH - 1))
    shift[p, CH - 1 + p // CH * CH] = 1.0
    anti = np.arange(CH)[None, :] == CH - 1 - (p % CH)[:, None]
    tables = {"rope": rope, "masks": masks, "ident": np.eye(P), "chan": chan, "srow": srow,
              "powers": powers, "signs": signs, "shift": shift, "anti": anti}
    return {k: np.ascontiguousarray(v, dtype=np.float32) for k, v in tables.items()}


SEMS = """
consts params x0 x1 weights l1_weights cweights
zeroed ones ct_ps ct_sb psel_ps psel_m abcd wbc powA expA es we e2w dg pre m2 m1_ps m1 upre_ps uw
negexp silu sil silrep modrep_ps modc_ps sel_ready clamp ln_nw
mods_ready modc_ready
ln_st ln_mv ln_ln ln_r ln_nb ln_x ln_m ln_h
hg_ps hg u_ps scan y_ps yg yt_ps y_t
t1_ps t1 t2_ps t2
wconl l1_cols hc_a ve_a g_hs_a buffers qk_ss ident_b mask_b rope_s
hc qk v tr sim pt pv ot wo_ps
qk_sq qk_ln qk_rn qkT v_sb ex ptT oT
qk_ssq qk_n qk_c qk_rot mx rinv on att_res
qk_s ve ones_v
g_hs g_tp g_st g_mv g_va g_r g_x g_tb g_h
m_gps m_g m_hid m_o m_res
c_cp c_qkv c_v c_max c_sub c_e c_sum c_rec c_qn c_kv c_t0 c_t c_qt c_o c_x3 wt_ps wt
d_up d_g d_dn d_y d_x4 d_ot d_o
bu_t bu_y bd_t bd_y bb_t bb_y wc_ps wc wd_ps wd bcol
held qk_nw
""".split()
Signals = namedtuple("Signals", SEMS)


def build(nc, a, out):
    with ExitStack() as ctx:
        ctx.enter_context(nc.allow_non_contiguous_dma(reason="columns of small vectors"))
        def sb(name, *shape, dt=F32):
            return ctx.enter_context(nc.sbuf_tensor(name, [P, *shape], dt))

        s = Signals(*(ctx.enter_context(nc.semaphore("s_" + n)) for n in SEMS))
        bw = [ctx.enter_context(nc.semaphore(f"s_bw{n}")) for n in range(2)]
        stored = [ctx.enter_context(nc.semaphore(f"s_stored{n}")) for n in range(2)]

        def wait(eng, signal, value):
            if not isinstance(value, int) or value > 0:
                eng.wait_ge(signal, value)

        PS = ctx.enter_context(nc.psum_tensor("PS", [P, 8, BANK], F32))

        ident, identb = sb("ident", P), sb("identb", P, dt=BF16)
        ropec = sb("ropec", TPB, 4, DH)
        maskb = sb("maskb", TPB + 1, P, dt=BF16)
        chan, srow = sb("chan", CG), sb("srow", P)
        powers, signs = sb("powers", CH + 1), sb("signs", CH + 1)
        shift, anti = sb("shift", P + CH - 1), sb("anti", CH)
        ones, mhalf = sb("ones", P), sb("mhalf", 8)
        cT, wmod = sb("cT", 2, B), sb("wmod", 2, 6 * D)
        C_col = sb("C_col", S)
        wqkv, wo = sb("wqkv", 3 * INNER), sb("wo", PAIRS, D)
        w1, w2 = sb("w1", 2 * HID), sb("w2", len(HT), D)
        qks, b1c, lgc = sb("qks", 2, DH), sb("b1c", 2, len(HT)), sb("lgc", 3)
        ropes = sb("ropes", TPB, 4, DH)
        wq1, wqkvT = sb("wq1", 3, D), sb("wqkvT", 3 * D)
        wcon, bexp, bcol, bcols = sb("wcon", 4, D), sb("bexp", HIDDEN), sb("bcol", 5), sb("bcols", 6)
        wu, wdT, wd = sb("wu", HIDDEN), sb("wdT", HIDDEN), sb("wd", 4, D)
        sil, silrep = sb("sil", 4, 2 * B), sb("silrep", 2, 2, P // 2)
        gar = sb("gar", 2, D)
        modc, gcol, gtmp = sb("modc", 2, 6, B), sb("gcol", 2, 2, B), sb("gtmp", 2, 4 * B)
        gtmr = sb("gtmr", 2, 2, D)

        XA, XB, X1 = sb("XA", B * PADN), sb("XB", B * PADN), sb("X1", TOK)
        arena = sb("arena", ARENA)

        def area(start, *shape, of=arena):
            names = "abcd"[:len(shape)]
            v = of[:, start:start + int(np.prod(shape))]
            if len(shape) > 1:
                v = v.rearrange(f"p ({' '.join(names)}) -> p {' '.join(names)}", **dict(zip(names[1:], shape[1:])))
            return v

        XP, HP = area(0, 2, CH, D), area(TOK, 2, D, CH)
        HG, HS = area(2 * TOK, G, 2 * P), area(3 * TOK, G, B, NCH + 1)
        YG, H2 = area(TOK, G, 2 * P), \
            area(2 * TOK, 2, CH, D)
        at = 4 * TOK + G * B
        UW, M1, M2 = area(at, G, P), area(at + G * P, G, P), area(at + 2 * G * P, G, P)
        upre = area(3 * TOK, G, CG, CH)
        A_row, B_row, D_row, C_row = (area(3 * PADN + 1 + n * D, D, of=XB) for n in range(4))
        bwr, cmp = area(0, 2, 4 * HIDDEN // 2, of=XB), area(2 * HIDDEN * 2, 2, HIDDEN, of=XB)
        maskf = area(at + 3 * G * P, TPB + 1, P)
        places, taken = [], 0
        for shape in ((4 * G, CG), (G, CH + 1), (G, CH + 1), (G, 2 * CH - 1), (G, CH), (G, CH), (2, CH, 32), (2, 3, D)):
            places.append(area(taken, *shape, of=X1))
            taken += int(np.prod(shape))
        assert taken <= TOK
        psel, ee, es, we, e2w, dg, ytmp, modr = places
        abcd, wbc, a16 = sb("abcd", 4, G), sb("wbc", G), sb("a16", G)
        stx, mvx, rsx = sb("stx", 2 * CH, 6), sb("mvx", 2 * CH, 2), sb("rsx", 3, 2 * CH)

        block = ctx.enter_context(nc.Block())

        out_rows = out.rearrange("b (t p) d -> (b t) p d", p=P)
        x_rows = a["L0_attn_x"].rearrange("b (k i) d -> (b k) (i d)", i=CH)

        N_CONST, N_PARAM, N_WEIGHT = 16 * 9, 16 * 8, 16 * 16

        def pe_state_space(pe):
            pe.wait_ge(s.consts, N_CONST - 32)
            pe.wait_ge(s.params, N_PARAM)
            pe.wait_ge(s.wconl, 16)
            for j in range(4):
                t = pe.transpose(PS[:, 7, j * P:(j + 1) * P], wcon[:, j, :], ident[:, :])
            t.then_inc(s.wc_ps, 1)
            pe.transpose(PS[0:S, 0, 0:P], C_col[:, :], ident[:, :]).then_inc(s.ct_ps, 1)
            pe.wait_ge(s.sil, 1)
            for l in range(2):
                for j in range(6):
                    last = pe.matmul(PS[:, 1, (l * 6 + j) * B:(l * 6 + j + 1) * B], wmod[:, l, j * D:(j + 1) * D],
                                     sil[:, 3, l * B:(l + 1) * B], start=True, stop=True)
            last.then_inc(s.modc_ps, 1)
            pe.wait_ge(s.silrep, 1)
            for h in range(2):
                last = pe.matmul(PS[:, 2 + h, 0:3 * D], silrep[:, h, :, :], wmod[:, 0, 0:3 * D], start=True, stop=True)
            last.then_inc(s.modrep_ps, 1)
            pe.wait_ge(s.ct_sb, 1)
            pe.wait_ge(s.ones, 1)
            for j, (w, v) in enumerate(((srow[0:S, :], A_row[0:S, :]), (srow[0:S, :], B_row[0:S, :]),
                                        (srow[0:S, :], C_row[0:S, :]), (ones[0:1, :], D_row[0:1, :]))):
                last = pe.matmul(PS[:, 0, j * D:(j + 1) * D], w, v, start=True, stop=True)
            last.then_inc(s.psel_ps, 1)
            pe.wait_ge(s.we, 1)
            pe.wait_ge(s.dg, 1)
            pe.wait_ge(s.modrep_ps, 1)
            for j in range(CH):
                pe.matmul(PS[:, 4, 0:G * CH], shift[:, CH - 1 - j:CH - 1 - j + P], we[:, :, j:j + CH], start=(j == 0), stop=False)
            pe.matmul(PS[:, 4, 0:G * CH], ident[:, :], dg[:, :, :], start=False, stop=True).then_inc(s.m1_ps, 1)
            pe.wait_ge(s.pre, 1)
            pe.wait_ge(s.wc, 1)
            pe.wait_ge(s.mods_ready, 1)
            pe.wait_ge(s.modc_ready, 1)
            for g in range(G):
                if g == 12:
                    pe.wait_ge(s.m1, 1)
                if g == 4:
                    pe.wait_ge(s.psel_m, 1)
                t = pe.transpose(PS[:, (5, 6, 7, 4)[g // 4], (g % 4) * P:(g % 4 + 1) * P], upre[:, g, :, :], ident[:, :])
                if g % 4 == 3:
                    t.then_inc(s.upre_ps, 1)
            for k in range(8):
                if k == 0:
                    pe.wait_ge(s.ln_h, 2)
                    pe.wait_ge(s.uw, 4)
                for g in (2 * k, 2 * k + 1):
                    for h in range(2):
                        t = pe.transpose(PS[:, k, ((g % 2) * 2 + h) * P:((g % 2) * 2 + h + 1) * P],
                                         HP[:, h, CG * g:CG * g + CG, :], ident[:, :])
                t.then_inc(s.hg_ps, 1)
            for k in range(8):
                pe.wait_ge(s.hg, k + 1)
                for g in (2 * k, 2 * k + 1):
                    t = pe.matmul(PS[:, k, (g % 2) * 2 * P:(g % 2 + 1) * 2 * P], UW[:, g, :], HG[:, g, :], start=True, stop=True)
                t.then_inc(s.u_ps, 1)
            for k in range(8):
                pe.wait_ge(s.scan, k + 1)
                if k == 0:
                    pe.wait_ge(s.m1, 1)
                    pe.wait_ge(s.m2, 1)
                for g in (2 * k, 2 * k + 1):
                    o = PS[:, k, (g % 2) * 2 * P:(g % 2 + 1) * 2 * P]
                    pe.matmul(o, M1[:, g, :], HG[:, g, :], start=True, stop=False)
                    t = pe.matmul(o, M2[:, g, :], HS[:, g, :, 0:NCH], start=False, stop=True)
                t.then_inc(s.y_ps, 1)
            for k in range(8):
                q, h = k // 2, k % 2
                pe.wait_ge(s.yg, 2 * q + 2)
                for g in range(4 * q, 4 * q + 4):
                    t = pe.transpose(PS[:, k, (g % 4) * P:(g % 4 + 1) * P], YG[:, g, h * P:(h + 1) * P], ident[:, :])
                t.then_inc(s.yt_ps, 1)
            for src, ps, free, ready in ((XP, s.t1_ps, None, s.y_t), (H2, s.t2_ps, s.t1, None)):
                for k in range(8):
                    h, q = k // 4, k % 4
                    if ready is not None:
                        pe.wait_ge(ready, 8)
                    else:
                        pe.wait_ge(s.ln_x, 2 * CH + CH * (h + 1))
                        pe.wait_ge(free, k + 1)
                    for i in range(4):
                        t = pe.transpose(PS[:, k, i * P:(i + 1) * P], src[:, h, 4 * q + i, :], ident[:, :])
                    t.then_inc(ps, 1)

        def stage_weights(eng):
            n = 0
            for name, order, users in (("L1_ffn_up_weights", range(STAGES), s.bb_y), ("L1_ffn_down_weights", reversed(range(STAGES)), s.bd_y)):
                for k in order:
                    if n >= 2:
                        eng.wait_ge(*((s.bb_y, n - 1) if n - 2 < STAGES else (s.bd_y, n - 1 - STAGES)))
                    eng.dma_start(bwr[:, n % 2, :], a[name][k:k + 1, :, :, :].rearrange("o w i j -> o (w i j)").to_broadcast([P, 2 * HIDDEN])).then_inc(bw[n % 2], 16)
                    n += 1

        def act_normalise(act, n, h, src, dst):
            r = slice(CH * h, CH * h + CH)
            act.wait_ge(s.ln_mv, 2 * n + h + 1)
            act.activation(rsx[:, 0, r], mvx[:, r, 1], ACT.Ln).then_inc(s.ln_ln, 1)
            act.wait_ge(s.ln_ln, 2 * n + h + 1)
            act.activation(rsx[:, 1, r], rsx[:, 0, r], ACT.Exp, scale=-0.5).then_inc(s.ln_r, 1)
            act.wait_ge(s.ln_nb, 2 * n + h + 1)
            for i in range(CH):
                act.activation(dst[:, h, :, i] if n == 0 else dst[:, h, i, :], src[:, h, i, :], ACT.Identity, bias=rsx[:, 2, CH * h + i:CH * h + i + 1],
                               scale=rsx[:, 1, CH * h + i:CH * h + i + 1]).then_inc(s.ln_x, 1)

        def act_state_space(act):
            act.preload_act_table_set("natural_log_exp_and_others")
            act.wait_ge(s.wc_ps, 1)
            act.activation(wdT[:, :], PS[:, 7, :], ACT.Copy).then_inc(s.wc, 1)
            act.wait_ge(s.params, N_PARAM)
            act.activation(sil[:, 0, :], cT[:, :, :].rearrange("p l b -> p (l b)"), ACT.Exp, scale=-1.0).then_inc(s.negexp, 1)
            act.wait_ge(s.powA, 1)
            act.activation(es[:, :, :], ee[:, :, :], ACT.Exp).then_inc(s.expA, 1)
            for h in range(2):
                act_normalise(act, 0, h, XP, HP)
            for k, bank in enumerate((5, 6, 7, 4)):
                act.wait_ge(s.upre_ps, k + 1)
                act.activation(UW[:, 4 * k:4 * k + 4, :], PS[:, bank, :].rearrange("p (g q) -> p g q", g=4), ACT.Copy).then_inc(s.uw, 1)
            for k in range(8):
                act.wait_ge(s.hg_ps, k + 1)
                act.activation(HG[:, 2 * k:2 * k + 2, :], PS[:, k, :].rearrange("p (g q) -> p g q", g=2), ACT.Copy).then_inc(s.hg, 1)
            for k in range(8):
                act.wait_ge(s.y_ps, k + 1)
                act.activation(YG[:, 2 * k:2 * k + 2, :], PS[:, k, :].rearrange("p (g q) -> p g q", g=2), ACT.Copy).then_inc(s.yg, 1)
            for k in range(8):
                h, q = k // 4, k % 4
                act.wait_ge(s.t1_ps, k + 1)
                o = X1[:, 2 * h * N:2 * (h + 1) * N].rearrange("p (b k i) -> p b k i", b=2, i=CH)[:, :, :, 4 * q:4 * q + 4]
                for b in range(2):
                    t = act.activation(o[:, b, :, :], PS[:, k, :].rearrange("p (i b k) -> p b k i", i=4, b=2)[:, b, :, :], ACT.Copy)
                t.then_inc(s.t1, 1)
            for h in range(2):
                act_normalise(act, 1, h, XP, H2)
            for k in range(8):
                h, q = k // 4, k % 4
                act.wait_ge(s.t2_ps, k + 1)
                for b in range(2):
                    bb = 2 * h + b
                    o = XA[:, bb * PADN + 1:(bb + 1) * PADN].rearrange("p (k i) -> p k i", i=CH)[:, :, 4 * q:4 * q + 4]
                    t = act.activation(o, PS[:, k, :].rearrange("p (i b k) -> p b k i", i=4, b=2)[:, b, :, :], ACT.Identity,
                                       bias=modc[:, 0, 3, bb:bb + 1], scale=modc[:, 0, 4, bb:bb + 1])
                t.then_inc(s.t2, 1)

        def dve_refine(dve, n, r):
            dve.tensor_tensor(rsx[:, 2, r], rsx[:, 1, r], rsx[:, 1, r], ALU.mult).then_inc(s.ln_nw, 1)
            dve.wait_ge(s.ln_nw, 3 * n + 1)
            dve.scalar_tensor_tensor(rsx[:, 2, r], rsx[:, 2, r], -0.5, mvx[:, r, 1], ALU.mult, ALU.mult).then_inc(s.ln_nw, 1)
            dve.wait_ge(s.ln_nw, 3 * n + 2)
            dve.scalar_tensor_tensor(rsx[:, 1, r], rsx[:, 2, r], 1.5, rsx[:, 1, r], ALU.add, ALU.mult).then_inc(s.ln_nw, 1)
            dve.wait_ge(s.ln_nw, 3 * n + 3)
            dve.scalar_tensor_tensor(rsx[:, 2, r], mvx[:, r, 0], -1.0, rsx[:, 1, r], ALU.mult, ALU.mult).then_inc(s.ln_nb, 1)

        def dve_statistics(dve, n, h):
            for i in range(CH * h, CH * h + CH):
                t = dve.bn_stats(stx[:, i, :], XP[:, h, i - CH * h, :])
            t.then_inc(s.ln_st, 1)
            dve.wait_ge(s.ln_st, 2 * n + h + 1)
            for i in range(CH * h, CH * h + CH):
                t = dve.bn_aggr(mvx[:, i, :], stx[:, i, :])
            t.then_inc(s.ln_m, 1)
            r = slice(CH * h, CH * h + CH)
            dve.wait_ge(s.ln_m, 2 * n + h + 1)
            dve.tensor_scalar(mvx[:, r, 1], mvx[:, r, 1], EPS, None, ALU.add).then_inc(s.ln_mv, 1)
            dve.wait_ge(s.ln_r, 2 * n + h + 1)
            dve_refine(dve, 2 * n + h, r)

        def dve_clamp(dve, out_ap, g_ap, t0, t1):
            dve.tensor_scalar(t0, g_ap, 0.0, 2.0, ALU.is_ge, ALU.mult).then_inc(s.clamp, 1)
            dve.scalar_tensor_tensor(t1, g_ap, -1.0, g_ap, ALU.mult, ALU.max).then_inc(s.clamp, 1)
            dve.wait_ge(s.clamp, clamps[0] + 2)
            dve.tensor_scalar(t1, t1, 0.25, None, ALU.max).then_inc(s.clamp, 1)
            clamps[0] += 4
            dve.wait_ge(s.clamp, clamps[0] - 1)
            return dve.scalar_tensor_tensor(out_ap, t0, -1.0, t1, ALU.add, ALU.mult).then_inc(s.clamp, 1)

        clamps = [0]

        def dve_state_space(dve):
            dve.wait_ge(s.negexp, 1)
            dve.tensor_scalar(sil[:, 1, :], sil[:, 0, :], 1.0, None, ALU.add).then_inc(s.silu, 1)
            dve.wait_ge(s.silu, 1)
            dve.reciprocal(sil[:, 2, :], sil[:, 1, :]).then_inc(s.silu, 1)
            dve.wait_ge(s.silu, 2)
            dve.tensor_tensor(sil[:, 3, :], sil[:, 2, :], cT[:, :, :].rearrange("p l b -> p (l b)"), ALU.mult).then_inc(s.sil, 1)
            dve.wait_ge(s.sil, 1)
            dve.tensor_copy(silrep[:, :, :, :].rearrange("p h b k -> p (h b) k"),
                            sil[:, 3, 0:B].unsqueeze(2).to_broadcast([P, B, P // 2])).then_inc(s.silrep, 1)
            dve.wait_ge(s.ct_ps, 1)
            dve.tensor_copy(C_row[0:S, :], PS[0:S, 0, 0:P]).then_inc(s.ct_sb, 1)
            dve.wait_ge(s.psel_ps, 1)
            dve.tensor_tensor(psel[:, :, :], PS[:, 0, :].rearrange("p (a c) -> p a c", c=CG),
                              chan[:, :].unsqueeze(1).to_broadcast([P, 4 * G, CG]), ALU.mult).then_inc(s.psel_m, 1)
            dve.wait_ge(s.psel_m, 1)
            dve.tensor_reduce(abcd[:, :, :].rearrange("p a g -> p (a g)"), psel[:, :, :], AX_X, ALU.add).then_inc(s.abcd, 1)
            dve.wait_ge(s.abcd, 1)
            dve.tensor_tensor(ee[:, :, :], abcd[:, 0, :].unsqueeze(2).to_broadcast([P, G, CH + 1]),
                              powers[:, :].unsqueeze(1).to_broadcast([P, G, CH + 1]), ALU.mult).then_inc(s.powA, 1)
            dve.tensor_tensor(wbc[:, :], abcd[:, 1, :], abcd[:, 2, :], ALU.mult).then_inc(s.wbc, 1)
            dve.memset(we[:, :, :], 0.0).then_inc(s.zeroed, 1)
            dve.tensor_tensor(dg[:, :, :], abcd[:, 3, :].unsqueeze(2).to_broadcast([P, G, CH]),
                              anti[:, :].unsqueeze(1).to_broadcast([P, G, CH]), ALU.mult).then_inc(s.dg, 1)
            dve.wait_ge(s.expA, 1)
            dve.tensor_tensor(es[:, :, :], es[:, :, :], signs[:, :].unsqueeze(1).to_broadcast([P, G, CH + 1]), ALU.mult).then_inc(s.es, 1)
            dve.wait_ge(s.es, 1)
            dve.wait_ge(s.wbc, 1)
            dve.wait_ge(s.zeroed, 1)
            wide = wbc[:, :].unsqueeze(2).to_broadcast([P, G, CH])
            dve.tensor_tensor(we[:, :, 0:CH], es[:, :, 1:CH + 1], wide, ALU.mult).then_inc(s.we, 1)
            dve.tensor_tensor(e2w[:, :, :], es[:, :, 0:CH], wide, ALU.mult).then_inc(s.e2w, 1)
            dve.tensor_copy(a16[:, :], es[:, :, 0]).then_inc(s.e2w, 1)
            blocks = chan[:, :].unsqueeze(1).unsqueeze(3).to_broadcast([P, G, CG, CH])
            dve.tensor_tensor(upre, es[:, :, 1:CH + 1].unsqueeze(2).to_broadcast([P, G, CG, CH]), blocks, ALU.mult).then_inc(s.pre, 1)
            dve.wait_ge(s.modc_ps, 1)
            dve.tensor_copy(modc[:, :, :, :].rearrange("p l j b -> p (l j b)"), PS[:, 1, 0:48]).then_inc(s.sel_ready, 1)
            dve.wait_ge(s.sel_ready, 1)
            gates = modc[:, :, 2:6:3, :].rearrange("p l j b -> p l j b")
            for l in range(2):
                for j in range(2):
                    dve_clamp(dve, gcol[:, l, j, :], modc[:, l, 2 + 3 * j, :], gtmp[:, 0, (2 * l + j) * B:(2 * l + j + 1) * B],
                              gtmp[:, 1, (2 * l + j) * B:(2 * l + j + 1) * B])
            for l in range(2):
                for j in (1, 4):
                    t = dve.tensor_scalar(modc[:, l, j, :], modc[:, l, j, :], 1.0, None, ALU.add)
            t.then_inc(s.modc_ready, 1)
            dve.wait_ge(s.modrep_ps, 1)
            for h in range(2):
                dve.tensor_copy(modr[:, h, 0:3, :].rearrange("p j d -> p (j d)"), PS[:, 2 + h, 0:3 * D]).then_inc(s.sel_ready, 1)
            dve.wait_ge(s.sel_ready, 3)
            for h in range(2):
                dve_clamp(dve, gar[:, h, :], modr[:, h, 2, :], gtmr[:, 0, h, :], gtmr[:, 1, h, :])
                t = dve.tensor_scalar(modr[:, h, 1, :], modr[:, h, 1, :], 1.0, None, ALU.add)
            t.then_inc(s.mods_ready, 1)
            dve.wait_ge(s.mods_ready, 1)
            for h, sx in enumerate((s.x0, s.x1)):
                dve.wait_ge(sx, 16)
                dve_statistics(dve, 0, h)
            dve.wait_ge(s.e2w, 2)
            dve.tensor_tensor(M2[:, :, :].rearrange("p g (c i) -> p g c i", c=CG), e2w[:, :, :].unsqueeze(2).to_broadcast([P, G, CG, CH]),
                              blocks, ALU.mult).then_inc(s.m2, 1)
            dve.wait_ge(s.m1_ps, 1)
            dve.tensor_tensor(M1[:, :, :].rearrange("p g (c i) -> p g c i", c=CG),
                              PS[:, 4, 0:G * CH].rearrange("p (g i) -> p g i", g=G).unsqueeze(2).to_broadcast([P, G, CG, CH]),
                              blocks, ALU.mult).then_inc(s.m1, 1)
            for h in range(2):
                dve.wait_ge(s.ln_x, CH * (h + 1))
                dve.tensor_tensor(HP[:, h, :, :], HP[:, h, :, :], modr[:, h, 1, :].unsqueeze(2).to_broadcast([P, D, CH]), ALU.mult).then_inc(s.sel_ready, 1)
                dve.wait_ge(s.sel_ready, 4 + h)
                dve.tensor_tensor(HP[:, h, :, :], HP[:, h, :, :], modr[:, h, 0, :].unsqueeze(2).to_broadcast([P, D, CH]), ALU.add).then_inc(s.ln_h, 1)
            dve.wait_ge(s.upre_ps, 4)
            dve.memset(HS[:, :, :, 0], 0.0).then_inc(s.zeroed, 1)
            for k in range(8):
                dve.wait_ge(s.u_ps, k + 1)
                for g in (2 * k, 2 * k + 1):
                    for b in range(B):
                        c0 = (g % 2) * 2 * P + b * NCH
                        t = dve.tensor_tensor_scan(HS[:, g, b, 1:NCH + 1], a16[:, g:g + 1].to_broadcast([P, NCH]),
                                                   PS[:, k, c0:c0 + NCH], 0.0, ALU.mult, ALU.add)
                t.then_inc(s.scan, 1)
            for k in range(8):
                q, h = k // 2, k % 2
                dve.wait_ge(s.yt_ps, k + 1)
                y = PS[:, k, :].rearrange("p (gc i) -> p i gc", i=CH)[:, ::-1, :]
                c = slice(32 * q, 32 * q + 32)
                dve.tensor_tensor(ytmp[:, k % 2, :, :], y, gar[:, h, c].unsqueeze(1).to_broadcast([P, CH, 32]), ALU.mult).then_inc(s.ln_m, 1)
                dve.wait_ge(s.ln_m, 2 + k + 1)
                dve.tensor_tensor(XP[:, h, :, c], XP[:, h, :, c], ytmp[:, k % 2, :, :], ALU.add).then_inc(s.y_t, 1)
            dve.wait_ge(s.y_t, 8)
            ln_m_base = 8
            for h in range(2):
                for i in range(CH * h, CH * h + CH):
                    t = dve.bn_stats(stx[:, i, :], XP[:, h, i - CH * h, :])
                t.then_inc(s.ln_st, 1)
                dve.wait_ge(s.ln_st, 2 + h + 1)
                for i in range(CH * h, CH * h + CH):
                    t = dve.bn_aggr(mvx[:, i, :], stx[:, i, :])
                t.then_inc(s.ln_m, 1)
                r = slice(CH * h, CH * h + CH)
                dve.wait_ge(s.ln_m, 2 + ln_m_base + h + 1)
                dve.tensor_scalar(mvx[:, r, 1], mvx[:, r, 1], EPS, None, ALU.add).then_inc(s.ln_mv, 1)
                dve.wait_ge(s.ln_r, 2 + h + 1)
                dve_refine(dve, 2 + h, r)

        def pool_setup(pool):
            pool.memset(ones[:, :], 1.0).then_inc(s.ones, 1)
            pool.memset(mhalf[:, :], -0.5).then_inc(s.ones, 1)
            pool.wait_ge(s.consts, N_CONST)
            pool.tensor_copy(identb[:, :], ident[:, :]).then_inc(s.ident_b, 1)
            pool.tensor_copy(maskb[:, :, :], maskf[:, :, :]).then_inc(s.mask_b, 1)
            pool_compose(pool)
            for t in (XA, XB):
                pool.memset(t[:, :].rearrange("p (b t) -> p b t", b=B)[:, :, 0], 0.0).then_inc(s.ones_v, 1)

        class Cut:
            def __init__(self, start=0):
                self.at = start

            def __call__(self, *shape):
                v = area(self.at, *shape)
                self.at += int(np.prod(shape))
                assert self.at <= ARENA
                return v

        cut = Cut()
        HC = cut(2, P)
        SQ, QN, QC, QS, QR = (cut(2, HEADS, DH) for _ in range(5))
        QB = cut(2, 2 * PAIRS, P)
        KT = cut(2, PAIRS, 3, WIN)
        EX = cut(2, 2 * PAIRS, P)
        PTs = cut(2 * PAIRS, P)
        VO, VE = cut(2, HEADS, DH + 1), cut(2, HEADS, DH + 1)
        ON, OT = cut(HEADS, DH), cut(2, PAIRS, P)
        nrm = sb("nrm", 4, 2 * HEADS)
        mxs, rin = sb("mxs", 2 * PAIRS), sb("rin", HEADS)
        HSG_AT = cut.at
        HSG, HNG, HFG = cut(2, BANK), cut(4, P), cut(2, BANK)
        GE, HD = cut(2, BANK), cut(len(HT), BANK)
        stg, mvg, rsg = sb("stg", 4, 6), sb("mvg", 4, 2), sb("rsg", 4)

        def batch(t, bits):
            b = t >> bits
            return b if isinstance(b, int) else b.with_bounds(max_val=B - 1)

        def tok(t):
            return t * P + batch(t, 3) + 1

        def gtok(m):
            return m * BANK + batch(m, 1) + 1

        def cols(start, n):
            return slice(start, start + n) if isinstance(start, int) else bass.ds(start, n)

        def within(eng, signal, base, k, most=None):
            if isinstance(k, int):
                k = k if most is None else min(k, most)
                if k <= 0:
                    return
            eng.wait_ge(signal, base + k)

        def hold(eng, signal):
            eng.sem_inc(signal, 1)

        def pipeline(eng, steps, last, stages, first_pair, pairs):
            def step(n, parity, inside):
                for lag, f in stages:
                    if inside or 0 <= n - lag < steps:
                        f(n - lag, (parity - lag) % 2)
            for n in range(-1, first_pair):
                step(n, n % 2, False)
            hold(eng, s.held)
            with eng.Fori(0, pairs) as q:
                for k in range(2):
                    step(q * 2 + (first_pair + k), (first_pair + k) % 2, True)
            for n in range(first_pair + 2 * pairs, last):
                step(n, n % 2, False)

        def pe_attention(pe, L):
            def qk(t, par):
                within(pe, s.hc, L, t + 1)
                within(pe, s.qk_n, L, t)
                pe.matmul(PS[:, 0, :], HC[:, par, :], wqkv[:, 0:INNER], start=True, stop=True)
                pe.matmul(PS[:, 1, :], HC[:, par, :], wqkv[:, INNER:2 * INNER], start=True, stop=True).then_inc(s.qk, 1)

            def v(t, par):
                within(pe, s.v_sb, L, t)
                within(pe, s.oT, L, t - 1)
                pe.matmul(PS[:, 6, :], HC[:, par, :], wqkv[:, 2 * INNER:3 * INNER], start=True, stop=True).then_inc(s.v, 1)

            def turn_qk(t, par):
                within(pe, s.qk_rot, L, t + 1)
                within(pe, s.ptT, L, t - 1)
                for j in range(2):
                    for hp in range(PAIRS):
                        x = pe.transpose(PS[:, 2 + j, hp * P:(hp + 1) * P], QR[:, j, 2 * hp:2 * hp + 2, :], ident[:, :])
                x.then_inc(s.tr, 1)

            def scores(t, par):
                within(pe, s.qkT, L, t + 1)
                within(pe, s.ex, L, t)
                for w in range(2):
                    m = maskb[:, cols(t & 7, 1), :] if w == 0 else maskb[:, TPB:TPB + 1, :]
                    pe.matmul(PS[:, 4 + w, :], identb[:, :], m.to_broadcast([P, PAIRS, P]), start=True, stop=False, skip_group_check=True)
                    for hp in range(PAIRS):
                        k = KT[:, par, hp, 0:2, :] if w == 0 else KT[:, par, hp, 0:3:2, :]
                        x = pe.matmul(PS[:, 4 + w, hp * P:(hp + 1) * P], QB[:, par, w * PAIRS + hp, :], k,
                                      start=False, stop=(hp == PAIRS - 1), skip_group_check=True)
                x.then_inc(s.sim, 1)

            def turn_p(t, par):
                within(pe, s.ex, L, t + 1)
                within(pe, s.qkT, L, t + 2, TILES)
                for k in range(2 * PAIRS):
                    x = pe.transpose(PS[:, 2 + k // PAIRS, (k % PAIRS) * P:(k % PAIRS + 1) * P], EX[:, par, k, :], ident[:, :])
                x.then_inc(s.pt, 1)

            def pv(t, par):
                within(pe, s.ptT, L, t + 1)
                within(pe, s.ve, L, t + 1)
                within(pe, s.v_sb, L, t + 2, TILES)
                within(pe, s.att_res, L, t)
                for w in range(2):
                    for h in range(HEADS):
                        x = pe.matmul(PS[WIN * w:WIN * w + WIN, 6 + h // 4, (h % 4) * (DH + 1):(h % 4 + 1) * (DH + 1)],
                                      PTs[:, w * PAIRS + h // 2, (h % 2) * WIN:(h % 2 + 1) * WIN],
                                      (VE, VO)[w][:, par, h, :], start=True, stop=True)
                x.then_inc(s.pv, 1)

            def turn_o(t, par):
                within(pe, s.on, L, t + 1)
                for hp in range(PAIRS):
                    x = pe.transpose(PS[:, 6, hp * P:(hp + 1) * P], ON[:, 2 * hp:2 * hp + 2, :], ident[:, :])
                x.then_inc(s.ot, 1)

            def project(t, par):
                within(pe, s.oT, L, t + 1)
                for hp in range(PAIRS):
                    x = pe.matmul(PS[:, 7, 0:P], wo[:, hp, :], OT[:, par, hp, :], start=(hp == 0), stop=(hp == PAIRS - 1))
                x.then_inc(s.wo_ps, 1)

            pipeline(pe, TILES, TILES + 3, ((0, qk), (3, turn_o), (1, turn_qk), (3, project), (1, v), (2, turn_p), (1, scores), (2, pv)), 5, 12)

        def act_attention(act, L):
            def turned_q(t, par):
                within(act, s.tr, L, t + 1)
                within(act, s.sim, L, t)
                for j in range(2):
                    rows = slice(DH * j, DH * j + DH)
                    act.activation(QB[rows, par, :, DH * j:DH * j + DH].rearrange("p (w h) q -> p w h q", w=2),
                                   PS[rows, 2, :].rearrange("p (h w q) -> p w h q", h=PAIRS, w=2), ACT.Copy)

            def turned_k(t, par):
                kt = PS[:, 3, :].rearrange("p (h w q) -> p h w q", h=PAIRS, w=2)
                act.activation(KT[:, par, :, 0:3:2, :], kt, ACT.Copy)
                act.activation(KT[:, 1 - par, :, 1, :], kt[:, :, 1, :], ACT.Copy).then_inc(s.qkT, 1)

            def values(t, par):
                within(act, s.v, L, t + 1)
                within(act, s.pv, L, t - 1)
                within(act, s.ve, L, t)
                act.activation(VO[:, par, :, 0:DH], PS[:, 6, :].rearrange("p (h d) -> p h d", h=HEADS), ACT.Copy).then_inc(s.v_sb, 1)

            def squares(t, par):
                within(act, s.qk, L, t + 1)
                within(act, s.qk_ssq, L, t)
                act.activation(SQ, PS[:, 0:2, :].rearrange("p j (h d) -> p j h d", h=HEADS), ACT.Square).then_inc(s.qk_sq, 1)

            def rnorm(t, par):
                within(act, s.qk_ssq, L, t + 1)
                act.activation(nrm[:, 1, :], nrm[:, 0, :], ACT.Ln, scale=SS_SCALE).then_inc(s.qk_ln, 1)
                within(act, s.qk_ln, L, t + 1)
                within(act, s.qk_n, L, t)
                act.activation(nrm[:, 2, :], nrm[:, 1, :], ACT.Exp, scale=-0.5).then_inc(s.qk_rn, 1)

            def turned_p(t, par):
                within(act, s.pt, L, t + 1)
                within(act, s.pv, L, t)
                act.activation(PTs, PS[:, 2:4, :].rearrange("p w (h q) -> p (w h) q", h=PAIRS), ACT.Copy).then_inc(s.ptT, 1)

            def exponentials(t, par):
                within(act, s.mx, L, t + 1)
                within(act, s.pt, L, t - 1)
                for k in range(2 * PAIRS):
                    x = act.activation(EX[:, par, k, :], PS[:, 4 + k // PAIRS, (k % PAIRS) * P:(k % PAIRS + 1) * P], ACT.Exp, bias=mxs[:, k:k + 1])
                x.then_inc(s.ex, 1)

            hold(act, s.held)
            act.preload_act_table_set("natural_log_exp_and_others")
            pipeline(act, TILES, TILES + 3, ((0, squares), (1, turned_q), (1, turned_k), (0, rnorm), (1, values), (2, turned_p), (1, exponentials)), 5, 12)

        def dve_attention(dve, L):
            def outputs(t, par):
                within(dve, s.pv, L, t + 1)
                o = PS[:, 6:8, 0:4 * (DH + 1)].rearrange("p b (h e) -> p b h e", h=4)
                dve.reciprocal(rin[:, :].rearrange("p (b h) -> p b h", b=2), o[:, :, :, DH]).then_inc(s.rinv, 1)
                within(dve, s.rinv, L, t + 1)
                within(dve, s.ot, L, t)
                dve.tensor_tensor(ON.rearrange("p (b h) d -> p b h d", b=2), o[:, :, :, 0:DH],
                                  rin[:, :].rearrange("p (b h) -> p b h", b=2).unsqueeze(3).to_broadcast([P, 2, 4, DH]), ALU.mult).then_inc(s.on, 1)

            def turned_o(t, par):
                within(dve, s.ot, L, t + 1)
                within(dve, s.wo_ps, L, t - 1)
                dve.tensor_copy(OT[:, par, :, :], PS[:, 6, :].rearrange("p (h q) -> p h q", h=PAIRS)).then_inc(s.oT, 1)

            def norms(t, par):
                within(dve, s.qk_sq, L, t + 1)
                within(dve, s.qk_ln, L, t)
                dve.tensor_reduce(nrm[:, 0, :], SQ.rearrange("p j h d -> p (j h) d"), AX_X, ALU.add).then_inc(s.qk_ss, 1)
                within(dve, s.qk_ss, L, t + 1)
                dve.tensor_scalar(nrm[:, 0, :], nrm[:, 0, :], 1e-24, None, ALU.max).then_inc(s.qk_ssq, 1)

            def normed(t, par):
                within(dve, s.qk_rn, L, t + 1)
                dve.tensor_tensor(nrm[:, 3, :], nrm[:, 2, :], nrm[:, 2, :], ALU.mult).then_inc(s.qk_nw, 1)
                within(dve, s.qk_nw, 3 * L, 3 * t + 1)
                dve.scalar_tensor_tensor(nrm[:, 3, :], nrm[:, 3, :], -0.5 * SS_SCALE, nrm[:, 0, :], ALU.mult, ALU.mult).then_inc(s.qk_nw, 1)
                within(dve, s.qk_nw, 3 * L, 3 * t + 2)
                dve.scalar_tensor_tensor(nrm[:, 3, :], nrm[:, 3, :], 1.5, nrm[:, 2, :], ALU.add, ALU.mult).then_inc(s.qk_nw, 1)
                within(dve, s.qk_nw, 3 * L, 3 * t + 3)
                within(dve, s.qk_s, L, t)
                within(dve, s.qk_c, L, t)
                dve.tensor_tensor(QN.rearrange("p j h d -> p (j h) d"), PS[:, 0:2, :].rearrange("p j (h d) -> p (j h) d", h=HEADS),
                                  nrm[:, 3, :].unsqueeze(2).to_broadcast([P, 2 * HEADS, DH]), ALU.mult).then_inc(s.qk_n, 1)

            def cosines(t, par):
                within(dve, s.qk_n, L, t + 1)
                within(dve, s.qk_rot, L, t)
                tab = ropes[:, cols(t & 7, 1), 0:2, :].rearrange("p t j d -> p (t j) d").unsqueeze(2).to_broadcast([P, 2, HEADS, DH])
                dve.tensor_tensor(QC, QN, tab, ALU.mult).then_inc(s.qk_c, 1)

            def rotated(t, par):
                within(dve, s.qk_s, L, t + 1)
                within(dve, s.qk_c, L, t + 1)
                within(dve, s.tr, L, t)
                halves = "p j h (x d) -> p (j h) x d"
                dve.tensor_tensor(QR.rearrange(halves, x=2), QC.rearrange(halves, x=2),
                                  QS.rearrange(halves, x=2)[:, :, ::-1, :], ALU.add).then_inc(s.qk_rot, 1)

            def residual(t, par):
                within(dve, s.wo_ps, L, t + 1)
                c = cols(tok(t), P)
                dve.tensor_tensor(XB[:, c], PS[:, 7, 0:P], XA[:, c], ALU.add).then_inc(s.att_res, 1)

            def maxima(t, par):
                within(dve, s.sim, L, t + 1)
                within(dve, s.ex, L, t)
                sc = PS[:, 4:6, :].rearrange("p w (h k) -> p (w h) k", h=PAIRS)
                dve.tensor_reduce(mxs[:, :], sc, AX_X, ALU.max, negate=True).then_inc(s.mx, 1)

            pipeline(dve, TILES, TILES + 3, ((3, outputs), (1, rotated), (3, turned_o), (0, norms), (3, residual), (0, normed), (0, cosines), (1, maxima)), 5, 12)

        def pool_attention(pool, L):
            def shifted(t, par):
                within(pool, s.v, L, t - 1)
                hold(pool, s.held)
                pool.tensor_copy(HC[0:64, par, :], XA[0:64, cols(tok(t), P)]).then_inc(s.hc_a, 1)
                within(pool, s.hc_a, L, t + 1)
                hold(pool, s.held)
                pool.tensor_copy(HC[64:128, par, :], XA[64:128, cols(tok(t) - 1, P)]).then_inc(s.hc, 1)
                within(pool, s.hc, L, t + 1)

            def even_values(t, par):
                within(pool, s.v_sb, L, t + 1)
                within(pool, s.pv, L, t - 1)
                hold(pool, s.held)
                pool.tensor_copy(VE[0:64, par, :, :], VO[0:64, par, :, :]).then_inc(s.ve_a, 1)
                within(pool, s.ve_a, L, t + 1)
                hold(pool, s.held)
                pool.tensor_copy(VE[64:128, par, :, :], VO[64:128, 1 - par, :, :]).then_inc(s.ve, 1)
                within(pool, s.ve, L, t + 1)

            def sines(t, par):
                within(pool, s.qk_n, L, t + 1)
                within(pool, s.qk_rot, L, t)
                tab = ropes[:, cols(t & 7, 1), 2:4, :].rearrange("p t j d -> p (t j) d").unsqueeze(2).to_broadcast([P, 2, HEADS, DH])
                pool.tensor_tensor(QS, QN, tab, ALU.mult).then_inc(s.qk_s, 1)

            pipeline(pool, TILES, TILES + 3, ((-1, shifted), (0, sines), (1, even_values)), 5, 12)

        def pe_turn(pe, base, m, par):
            within(pe, s.g_hs, base, m + 1)
            within(pe, s.g_x, base, m)
            for i in range(4):
                x = pe.transpose(PS[:, 5, i * P:(i + 1) * P], HSG[:, par, i * P:(i + 1) * P], ident[:, :])
            x.then_inc(s.g_tp, 1)

        def pe_turn_back(pe, base, m, par):
            within(pe, s.g_x, base, m + 1)
            within(pe, s.g_h, base, m)
            for i in range(4):
                x = pe.transpose(PS[:, 6, i * P:(i + 1) * P], HNG[:, i, :], ident[:, :])
            x.then_inc(s.g_tb, 1)

        def dve_stats(dve, base, m, par):
            within(dve, s.g_tp, base, m + 1)
            for i in range(4):
                x = dve.bn_stats(stg[:, i, :], PS[:, 5, i * P:(i + 1) * P])
            x.then_inc(s.g_st, 1)
            within(dve, s.g_st, base, m + 1)
            within(dve, s.g_x, base, m)
            hold(dve, s.held)
            for i in range(4):
                x = dve.bn_aggr(mvg[:, i, :], stg[:, i, :])
            x.then_inc(s.g_mv, 1)
            within(dve, s.g_mv, base, m + 1)
            dve.tensor_scalar(mvg[:, :, 1], mvg[:, :, 1], EPS, None, ALU.add).then_inc(s.g_va, 1)

        def pool_rstd(pool, base, m, par):
            within(pool, s.g_va, base, m + 1)
            pool.tensor_tensor(rsg[:, :], mvg[:, :, 1], mhalf[:, 0:4], ALU.pow).then_inc(s.g_r, 1)

        def dve_center(dve, base, m, par):
            within(dve, s.g_r, base, m + 1)
            within(dve, s.g_tb, base, m)
            for i in range(4):
                x = dve.tensor_scalar(HNG[:, i, :], PS[:, 5, i * P:(i + 1) * P], mvg[:, i, 0:1], rsg[:, i:i + 1], ALU.subtract, ALU.mult)
            x.then_inc(s.g_x, 1)

        NH = len(HT)

        def pe_ffn(pe, base):
            def up(m, par):
                within(pe, s.g_h, base, m + 1)
                for j, (row, k) in enumerate(HT):
                    pr = 2 * ((NH * par + j) % 2)
                    within(pe, s.m_hid, base * NH, m * NH + j - 1)
                    pe.matmul(PS[0:k, pr, :], w1[:, row:row + k], HFG[:, par, :], start=True, stop=True)
                    pe.matmul(PS[0:k, pr + 1, :], w1[:, HID + row:HID + row + k], HFG[:, par, :], start=True, stop=True).then_inc(s.m_gps, 1)

            def down(m, par):
                within(pe, s.m_hid, base * NH, m * NH + NH)
                within(pe, s.m_res, base, m)
                for j, (row, k) in enumerate(HT):
                    x = pe.matmul(PS[:, 4, :], w2[0:k, j, :], HD[0:k, j, :], start=(j == 0), stop=(j == NH - 1))
                x.then_inc(s.m_o, 1)

            pipeline(pe, GROUPS, GROUPS + 1, ((0, lambda m, p: pe_turn(pe, base, m, p)), (1, up),
                                              (0, lambda m, p: pe_turn_back(pe, base, m, p)), (1, down)), 3, 2)

        def act_ffn(act, base):
            def gelus(m, par):
                for j, (row, k) in enumerate(HT):
                    x = (NH * par + j) % 2
                    within(act, s.m_gps, base * NH, m * NH + j + 1)
                    within(act, s.m_hid, base * NH, m * NH + j - 1)
                    act.activation(GE[0:k, x, :], PS[0:k, 2 * x + 1, :], ACT.Gelu, bias=b1c[0:k, 1, j:j + 1]).then_inc(s.m_g, 1)

            def scaled(m, par):
                within(act, s.g_tb, base, m + 1)
                within(act, s.m_o, base, m - 1)
                act.activation(HFG[:, par, :], PS[:, 6, :], ACT.Identity, bias=lgc[:, 1:2], scale=lgc[:, 0:1]).then_inc(s.g_h, 1)

            pipeline(act, GROUPS, GROUPS + 1, ((1, gelus), (0, scaled)), 3, 2)

        def dve_ffn(dve, base):
            def hidden(j):
                def f(m, par):
                    k = HT[j][1]
                    x = (NH * par + j) % 2
                    within(dve, s.m_g, base * NH, m * NH + j + 1)
                    within(dve, s.m_o, base, m)
                    dve.scalar_tensor_tensor(HD[0:k, j, :], PS[0:k, 2 * x, :], b1c[0:k, 0, j:j + 1], GE[0:k, x, :], ALU.add, ALU.mult).then_inc(s.m_hid, 1)
                return f

            def residual(m, par):
                within(dve, s.m_o, base, m + 1)
                c = cols(gtok(m), BANK)
                dve.scalar_tensor_tensor(XA[:, c], PS[:, 4, :], lgc[:, 2:3], XB[:, c], ALU.add, ALU.add).then_inc(s.m_res, 1)

            pipeline(dve, GROUPS, GROUPS + 1, ((0, lambda m, p: dve_stats(dve, base, m, p)), (1, hidden(0)),
                                               (0, lambda m, p: dve_center(dve, base, m, p)), (1, hidden(1)), (1, hidden(2)), (1, residual)), 3, 2)

        def pool_ffn(pool, base):
            def shifted(m, par):
                within(pool, s.g_tp, base, m - 1)
                hold(pool, s.held)
                pool.tensor_copy(HSG[0:64, par, :], XB[0:64, cols(gtok(m), BANK)]).then_inc(s.g_hs_a, 1)
                within(pool, s.g_hs_a, base, m + 1)
                hold(pool, s.held)
                pool.tensor_copy(HSG[64:128, par, :], XB[64:128, cols(gtok(m) - 1, BANK)]).then_inc(s.g_hs, 1)
                within(pool, s.g_hs, base, m + 1)

            pipeline(pool, GROUPS, GROUPS + 1, ((-1, shifted), (0, lambda m, p: pool_rstd(pool, base, m, p))), 3, 2)

        def nothing(*_):
            pass

        def attention_layers(eng, attention, ffn, start=nothing, each=nothing):
            eng.wait_ge(s.t2, 8)
            start(eng)
            with eng.Fori(0, DEPTH) as l:
                eng.wait_ge(s.weights, l * N_WEIGHT + N_WEIGHT)
                each(eng, l)
                attention(eng, l * TILES)
                eng.wait_ge(s.att_res, l * TILES + TILES)
                ffn(eng, l * GROUPS)
                eng.wait_ge(s.m_res, l * GROUPS + GROUPS)
                hold(eng, s.held)

        def dve_rope(dve, l):
            dve.wait_ge(s.consts, N_CONST)
            dve.tensor_tensor(ropes[:, :, :, :].rearrange("p t (x j) d -> p (t x) (j d)", x=2),
                              ropec[:, :, :, :].rearrange("p t (x j) d -> p (t x) (j d)", x=2),
                              qks[:, :, :].rearrange("p j d -> p (j d)").unsqueeze(1).to_broadcast([P, 2 * TPB, 2 * DH]), ALU.mult).then_inc(s.rope_s, 1)

        def pool_start(pool):
            pool.memset(QB, 0.0).then_inc(s.buffers, 1)
            pool.memset(KT, 0.0).then_inc(s.buffers, 1)
            pool.memset(VO, 0.0).then_inc(s.buffers, 1)
            pool.wait_ge(s.buffers, 3)
            pool.memset(VO[:, :, :, DH], 1.0).then_inc(s.buffers, 1)

        def with_buffers(eng):
            eng.wait_ge(s.buffers, 4)
            eng.wait_ge(s.ones, 2)
            eng.wait_ge(s.ones_v, 2)
            eng.wait_ge(s.ident_b, 1)
            eng.wait_ge(s.mask_b, 1)

        def pool_rope(pool, l):
            pool.wait_ge(s.rope_s, l + 1)

        H1 = D // HD1
        cut4 = Cut()
        QKE, VT = cut4(4, 2, D), cut4(4, D)
        KV, KVs = cut4(2, H1, HD1 * HD1), cut4(2, HD1 * HD1)
        TT, QT = cut4(2, HD1 * HD1), cut4(2, HD1, D)
        MX, ZS, ZI = cut4(4, H1 + HD1), cut4(4, H1 + HD1), cut4(4, H1 + HD1)
        assert cut4.at <= HSG_AT
        Q0 = DEPTH * GROUPS

        def token_tile(m, i):
            return m * 4 + i

        def pe_linear(pe):
            pe.wait_ge(s.l1_weights, 16 * 3)
            pe.wait_ge(s.m_res, DEPTH * GROUPS)
            for j in range(3):
                x = pe.transpose(PS[:, 0, j * P:(j + 1) * P], wq1[:, j, :], ident[:, :])
            x.then_inc(s.wt_ps, 1)
            pe.wait_ge(s.wt, 1)

            def qkv(m, par):
                within(pe, s.g_h, Q0, m + 1)
                within(pe, s.c_sub, 0, m * 2)
                within(pe, s.c_v, 0, m)
                for i in range(4):
                    x = pe.matmul(PS[:, i, 0:3 * D], HFG[:, par, i * P:(i + 1) * P], wqkvT[:, :], start=True, stop=True)
                x.then_inc(s.c_qkv, 1)

            def summed(m, par):
                within(pe, s.c_x3, 0, m - 1)
                for i in range(4):
                    within(pe, s.c_qt, 0, m * 4 + (i + 1))
                    for d in range(HD1):
                        x = pe.matmul(PS[:, (4, 7)[par], i * P:(i + 1) * P], QT[:, i % 2, d, :], ident[:, :], start=(d == 0), stop=(d == HD1 - 1))
                    x.then_inc(s.c_o, 1)

            pipeline(pe, GROUPS, GROUPS + 1, ((0, lambda m, p: pe_turn(pe, Q0, m, p)), (1, qkv),
                                              (0, lambda m, p: pe_turn_back(pe, Q0, m, p)), (1, summed)), 3, 2)

        def act_linear(act):
            act.wait_ge(s.wt_ps, 1)
            act.activation(wqkvT[:, :], PS[:, 0, 0:3 * P], ACT.Copy).then_inc(s.wt, 1)

            def kept(m, par):
                within(act, s.g_hs, Q0, m + 1)
                hold(act, s.held)
                act.activation(X1[:, cols(m * BANK, BANK)], HSG[:, par, :], ACT.Copy).then_inc(s.c_cp, 1)

            def scaled(m, par):
                within(act, s.g_tb, Q0, m + 1)
                within(act, s.c_qkv, 0, m - 1)
                b = bass.ds(batch(m, 1), 1)
                hold(act, s.held)
                act.activation(HFG[:, par, :], PS[:, 6, :], ACT.Identity, bias=modc[:, 1, 0, b], scale=modc[:, 1, 1, b]).then_inc(s.g_h, 1)

            def exponentials(m, par):
                within(act, s.c_qkv, 0, m + 1)
                within(act, s.c_kv, 0, m * 4)
                within(act, s.c_sub, 0, m * 2 + 2)
                act.activation(VT, PS[:, 0:4, 2 * D:3 * D], ACT.Copy).then_inc(s.c_v, 1)
                act.activation(QKE, QKE, ACT.Exp).then_inc(s.c_e, 1)

            pipeline(act, GROUPS, GROUPS + 1, ((-1, kept), (1, exponentials), (0, scaled)), 3, 2)

        def dve_linear(dve):
            def input_group(m, par):
                within(dve, s.g_tp, Q0, m - 1)
                within(dve, s.c_cp, 0, m - 1)
                b = batch(m, 1)
                dve.scalar_tensor_tensor(HSG[:, par, :], XA[:, cols(gtok(m), BANK)], gcol[:, 0, 1, cols(b, 1)],
                                         X1[:, cols(m * BANK, BANK)], ALU.mult, ALU.add).then_inc(s.g_hs, 1)

            def by_softmax(v):
                return v[:, :, 0, :].rearrange("p i (h d) -> p i h d", d=HD1), v[:, :, 1, :].rearrange("p i (h d) -> p i d h", d=HD1)

            def spread(v):
                return v[:, :, 0:H1].unsqueeze(3).to_broadcast([P, 4, H1, HD1]), v[:, :, H1:].unsqueeze(3).to_broadcast([P, 4, HD1, H1])

            logits = PS[:, 0:4, 0:2 * D].rearrange("p i (j c) -> p i j c", j=2)

            def maxima(m, par):
                within(dve, s.c_qkv, 0, m + 1)
                for part, x in zip((slice(0, H1), slice(H1, H1 + HD1)), by_softmax(logits)):
                    y = dve.tensor_reduce(MX[:, :, part], x, AX_X, ALU.max)
                y.then_inc(s.c_max, 1)
                within(dve, s.c_max, 0, m + 1)
                within(dve, s.c_qn, 0, m)
                within(dve, s.c_qt, 0, m * 4)
                for o, x, y in zip(by_softmax(QKE), by_softmax(logits), spread(MX)):
                    dve.tensor_tensor(o, x, y, ALU.subtract).then_inc(s.c_sub, 1)

            def sums(m, par):
                within(dve, s.c_e, 0, m + 1)
                for part, x in zip((slice(0, H1), slice(H1, H1 + HD1)), by_softmax(QKE)):
                    y = dve.tensor_reduce(ZS[:, :, part], x, AX_X, ALU.add)
                y.then_inc(s.c_sum, 1)
                within(dve, s.c_sum, 0, m + 1)
                dve.reciprocal(ZI, ZS).then_inc(s.c_rec, 1)
                within(dve, s.c_rec, 0, m + 1)
                q = by_softmax(QKE)[0]
                dve.tensor_tensor(q, q, spread(ZI)[0], ALU.mult).then_inc(s.c_qn, 1)

            def products(m, par):
                within(dve, s.c_v, 0, m + 1)
                for i in range(4):
                    dve.tensor_tensor(KV[:, i % 2, :, :].rearrange("p h (d e) -> p h d e", e=HD1),
                                      QKE[:, i, 1, :].rearrange("p (h d) -> p h d", d=HD1).unsqueeze(3).to_broadcast([P, H1, HD1, HD1]),
                                      VT[:, i, :].rearrange("p (h e) -> p h e", e=HD1).unsqueeze(2).to_broadcast([P, H1, HD1, HD1]),
                                      ALU.mult).then_inc(s.c_kv, 1)
                    if i > 0:
                        scaled_sum(m, i - 1)
                    within(dve, s.c_kv, 0, m * 4 + (i + 1))
                    dve.tensor_reduce(KVs[:, i % 2, :], KV[:, i % 2, :, :].rearrange("p h c -> p c h"), AX_X, ALU.add).then_inc(s.c_t0, 1)
                scaled_sum(m, 3)

            def scaled_sum(m, i):
                within(dve, s.c_t0, 0, m * 4 + (i + 1))
                within(dve, s.c_qt, 0, m * 4 + (i - 1))
                dve.tensor_tensor(TT[:, i % 2, :].rearrange("p (d e) -> p d e", e=HD1), KVs[:, i % 2, :].rearrange("p (d e) -> p d e", e=HD1),
                                  ZI[:, i, H1:].unsqueeze(2).to_broadcast([P, HD1, HD1]), ALU.mult).then_inc(s.c_t, 1)

            def residual(m, par):
                within(dve, s.c_o, 0, m * 4 + 4)
                within(dve, s.c_cp, 0, m + 1)
                c = cols(m * BANK, BANK)
                dve.scalar_tensor_tensor(X1[:, c], PS[:, (4, 7)[par], :], gcol[:, 1, 0, cols(batch(m, 1), 1)], X1[:, c], ALU.mult, ALU.add).then_inc(s.c_x3, 1)

            pipeline(dve, GROUPS, GROUPS + 2, ((-1, input_group), (0, lambda m, p: dve_stats(dve, Q0, m, p)), (1, maxima),
                                               (0, lambda m, p: dve_center(dve, Q0, m, p)), (1, sums), (1, products), (2, residual)), 3, 2)

        def pool_linear(pool):
            def products(m, par):
                within(pool, s.c_qn, 0, m + 1)
                for i in range(4):
                    within(pool, s.c_t, 0, m * 4 + (i + 1))
                    within(pool, s.c_o, 0, m * 4 + (i - 1))
                    pool.tensor_tensor(QT[:, i % 2, :, :].rearrange("p d (h e) -> p d h e", e=HD1),
                                       QKE[:, i, 0, :].rearrange("p (h d) -> p d h", d=HD1).unsqueeze(3).to_broadcast([P, HD1, H1, HD1]),
                                       TT[:, i % 2, :].rearrange("p (d e) -> p d e", e=HD1).unsqueeze(2).to_broadcast([P, HD1, H1, HD1]),
                                       ALU.mult).then_inc(s.c_qt, 1)

            pipeline(pool, GROUPS, GROUPS + 1, ((0, lambda m, p: pool_rstd(pool, Q0, m, p)), (1, products)), 3, 2)

        cut5 = Cut()
        GD, YD, XF, OB = cut5(2, 4, BANK), cut5(BANK), cut5(2, BANK), cut5(2, 4, P)
        Q1 = Q0 + GROUPS

        def pe_butterfly(pe):
            pe.wait_ge(s.c_x3, GROUPS)
            pe.wait_ge(s.bd_y, STAGES)
            for j in range(4):
                x = pe.transpose(PS[:, 0, j * P:(j + 1) * P], wdT[:, j * P:(j + 1) * P], ident[:, :])
            x.then_inc(s.wd_ps, 1)
            pe.wait_ge(s.bb_y, STAGES)
            for j in range(4):
                x = pe.matmul(PS[:, 1, j:j + 1], bexp[0:1, j * P:(j + 1) * P], ones[0:1, 0:1], start=True, stop=True)
            x.then_inc(s.wd_ps, 1)
            pe.wait_ge(s.wd, 2)

            def up(m, par):
                within(pe, s.g_h, Q1, m + 1)
                for j in range(4):
                    within(pe, s.d_g, 0, m * 4 + (j - 3))
                    pe.matmul(PS[:, j, :], wu[:, j * P:(j + 1) * P], HFG[:, par, :], start=True, stop=True).then_inc(s.d_up, 1)

            def down(m, par):
                within(pe, s.d_g, 0, m * 4 + 4)
                within(pe, s.d_y, 0, m)
                for j in range(4):
                    x = pe.matmul(PS[:, 4, :], wd[:, j, :], GD[:, par, j, :], start=(j == 0), stop=(j == 3))
                x.then_inc(s.d_dn, 1)

            def turn_out(m, par):
                within(pe, s.d_x4, 0, m + 1)
                within(pe, s.d_o, 0, m)
                for i in range(4):
                    x = pe.transpose(PS[:, 7, i * P:(i + 1) * P], XF[:, par, i * P:(i + 1) * P], ident[:, :])
                x.then_inc(s.d_ot, 1)

            pipeline(pe, GROUPS, GROUPS + 2, ((0, lambda m, p: pe_turn(pe, Q1, m, p)), (1, up),
                                              (0, lambda m, p: pe_turn_back(pe, Q1, m, p)), (2, turn_out), (1, down)), 4, 2)

        def act_butterfly(act):
            act.wait_ge(s.wd_ps, 1)
            act.activation(wd[:, :, :], PS[:, 0, :].rearrange("p (j d) -> p j d", j=4), ACT.Copy).then_inc(s.wd, 1)

            def gelus(m, par):
                for j in range(4):
                    within(act, s.d_up, 0, m * 4 + j + 1)
                    within(act, s.d_dn, 0, m - 1)
                    act.activation(GD[:, par, j, :], PS[:, j, :], ACT.Gelu, bias=bcol[:, j:j + 1]).then_inc(s.d_g, 1)

            def scaled(m, par):
                within(act, s.g_tb, Q1, m + 1)
                within(act, s.d_up, 0, (m - 1) * 4)
                b = bass.ds(batch(m, 1), 1)
                hold(act, s.held)
                act.activation(HFG[:, par, :], PS[:, 6, :], ACT.Identity, bias=modc[:, 1, 3, b], scale=modc[:, 1, 4, b]).then_inc(s.g_h, 1)

            def outputs(m, par):
                within(act, s.d_ot, 0, m + 1)
                within(act, stored[par], 0, (m >> 1) * 16)
                act.activation(OB[:, par, :, :], PS[:, 7, :].rearrange("p (i d) -> p i d", i=4), ACT.Copy).then_inc(s.d_o, 1)

            pipeline(act, GROUPS, GROUPS + 2, ((1, gelus), (0, scaled), (2, outputs)), 4, 2)

        def dve_butterfly(dve):
            dve.wait_ge(s.l1_cols, 16 * 3)
            dve.wait_ge(s.wd_ps, 2)
            dve.tensor_tensor(bcol[:, 0:4], PS[:, 1, 0:4], bcols[:, 0:4], ALU.add).then_inc(s.wd, 1)
            dve.tensor_tensor(bcol[:, 4:5], bcols[:, 4:5], bcols[:, 5:6], ALU.add).then_inc(s.bcol, 1)
            dve.wait_ge(s.bcol, 1)

            def gated(m, par):
                within(dve, s.d_dn, 0, m + 1)
                within(dve, s.d_x4, 0, m)
                dve.tensor_scalar(YD, PS[:, 4, :], bcol[:, 4:5], gcol[:, 1, 1, cols(batch(m, 1), 1)], ALU.add, ALU.mult).then_inc(s.d_y, 1)
                within(dve, s.d_y, 0, m + 1)
                within(dve, s.d_ot, 0, m - 1)
                dve.tensor_tensor(XF[:, par, :], YD, X1[:, cols(m * BANK, BANK)], ALU.add).then_inc(s.d_x4, 1)

            pipeline(dve, GROUPS, GROUPS + 2, ((0, lambda m, p: dve_stats(dve, Q1, m, p)), (0, lambda m, p: dve_center(dve, Q1, m, p)), (1, gated)), 4, 2)

        def pool_butterfly(pool):
            def taken(m, par):
                within(pool, s.g_tp, Q1, m - 1)
                pool.wait_ge(s.c_x3, GROUPS)
                hold(pool, s.held)
                pool.tensor_copy(HSG[:, par, :], X1[:, cols(m * BANK, BANK)]).then_inc(s.g_hs, 1)

            pipeline(pool, GROUPS, GROUPS + 2, ((-1, taken), (0, lambda m, p: pool_rstd(pool, Q1, m, p))), 2, 2)

        def pool_compose(pool):
            def stage(rows, y, w, transposed, k, t_done, y_done):
                st = 1 << k
                w = w[rows].rearrange("p (n q o i) -> p n q o i", q=st, o=2, i=2)
                y = y[rows].rearrange("p (n h q) -> p n h q", h=2, q=st)
                for h in range(2):
                    part = (w[:, :, :, h, :] if transposed else w[:, :, :, :, h]).rearrange("p n q o -> p n o q")
                    o = cmp[rows, h, :].rearrange("p (n h q) -> p n h q", h=2, q=st)
                    for f in range(2):
                        pool.tensor_tensor(o[:, :, f, :], y[:, :, h, :], part[:, :, f, :], ALU.mult).then_inc(t_done, 1)
                pool.wait_ge(t_done, 4 * (counts[t_done.name] + 1))
                pool.tensor_tensor(y.rearrange("p n h q -> p (n h q)"), cmp[rows, 0, :], cmp[rows, 1, :], ALU.add).then_inc(y_done, 1)
                counts[t_done.name] += 1
                pool.wait_ge(y_done, counts[t_done.name])
            counts = {s.bu_t.name: 0, s.bd_t.name: 0, s.bb_t.name: 0}
            pool.wait_ge(s.cweights, 16 * 2)
            n = 0
            for k in range(STAGES):
                pool.wait_ge(bw[n % 2], 16 * (n // 2 + 1))
                stage(slice(0, P), wu[:, :], bwr[:, n % 2, :], False, k, s.bu_t, s.bu_y)
                stage(slice(0, 1), bexp[:, :], bwr[:, n % 2, :], False, k, s.bb_t, s.bb_y)
                n += 1
            pool.wait_ge(s.wc, 1)
            for k in reversed(range(STAGES)):
                pool.wait_ge(bw[n % 2], 16 * (n // 2 + 1))
                stage(slice(0, P), wdT[:, :], bwr[:, n % 2, :], True, k, s.bd_t, s.bd_y)
                n += 1
        @block.sync
        def _(sp):
            for t, name in ((ident, "ident"), (srow, "srow"), (chan, "chan"), (powers, "powers"), (signs, "signs"), (anti, "anti")):
                sp.dma_start(t[:, :], a[name]).then_inc(s.consts, 16)
            sp.dma_start(shift[:, :], a["shift"]).then_inc(s.consts, 16)
            sp.dma_start(A_row[0:S, :], a["L0_attn_A_log"]).then_inc(s.params, 16)
            sp.dma_start(B_row[0:S, :], a["L0_attn_B"]).then_inc(s.params, 16)
            sp.dma_start(C_col[:, :], a["L0_attn_C"]).then_inc(s.params, 16)
            sp.dma_start(D_row[0:1, :], a["L0_attn_D"].rearrange("(o d) -> o d", o=1)).then_inc(s.params, 16)
            for n, pre in enumerate(("L0", "L1")):
                sp.dma_start(cT[:, n, :], a[pre + "_c"].rearrange("b k -> k b")).then_inc(s.params, 16)
                sp.dma_start(wmod[:, n, :], a[pre + "_wmod"]).then_inc(s.params, 16)
            for h, sx in enumerate((s.x0, s.x1)):
                sp.dma_start(XP[:, h, :, :], x_rows[P * h:P * h + P, :].rearrange("p (i d) -> p i d", i=CH)).then_inc(sx, 16)
            sp.dma_start(ropec[:, :, :, :], a["rope"].rearrange("p t (f d) -> p t f d", f=4)).then_inc(s.consts, 16)
            sp.dma_start(maskf[:, :, :], a["masks"]).then_inc(s.consts, 16)
            sp.dma_start(wcon[:, :, :], a["L1_ffn_W_con"].rearrange("(j p) d -> p j d", p=P)).then_inc(s.wconl, 16)
            sp.dma_start(wu[:, :], a["L1_ffn_W_exp"]).then_inc(s.cweights, 16)
            sp.dma_start(bexp[0:1, :], a["L1_ffn_b_exp"].rearrange("(o d) -> o d", o=1)).then_inc(s.cweights, 16)
            sp.dma_start(bcols[:, 0:4], a["L1_ffn_up_bias"].rearrange("(j p) -> p j", p=P)).then_inc(s.l1_cols, 16)
            for j, name in enumerate(("L1_ffn_b_con", "L1_ffn_down_bias")):
                sp.dma_start(bcols[:, 4 + j:5 + j], a[name].rearrange("(p o) -> p o", o=1)).then_inc(s.l1_cols, 16)
            for j, name in enumerate(("L1_attn_W_Q", "L1_attn_W_K", "L1_attn_W_V")):
                sp.dma_start(wq1[:, j, :], a[name]).then_inc(s.l1_weights, 16)
            stage_weights(sp)
            with sp.Fori(0, DEPTH) as l:
                one = bass.ds(l, 1)
                sp.dma_start(wqkv[:, :], a["L0_ffn_wqkv"][one, :, :].rearrange("o k n -> k (o n)")).then_inc(s.weights, 16)
                sp.dma_start(wo[:, :, :], a["L0_ffn_wo"][one, :, :].rearrange("o (t p) n -> p (o t) n", p=P)).then_inc(s.weights, 16)
                sp.dma_start(w1[:, :], a["L0_ffn_w1"][one, :, :].rearrange("o k n -> k (o n)")).then_inc(s.weights, 16)
                sp.dma_start(w2[:, 0:2, :], a["L0_ffn_w2"][one, 0:2 * P, :].rearrange("o (t p) n -> p (o t) n", p=P)).then_inc(s.weights, 16)
                sp.dma_start(w2[0:HID - 2 * P, 2, :], a["L0_ffn_w2"][one, 2 * P:HID, :].rearrange("o p n -> p (o n)")).then_inc(s.weights, 16)
                for j, name in enumerate(("L0_ffn_q_scale", "L0_ffn_k_scale")):
                    sp.dma_start(qks[:, j, :], a[name][one, :].to_broadcast([P, DH])).then_inc(s.weights, 16)
                for j, name in enumerate(("L0_ffn_ln_g", "L0_ffn_ln_b", "L0_ffn_b2")):
                    sp.dma_start(lgc[:, j:j + 1], a[name][one, :].rearrange("o d -> d o")).then_inc(s.weights, 16)
                for half in range(2):
                    for t, (j, k) in enumerate(HT):
                        col = half * HID + j
                        sp.dma_start(b1c[0:k, half, t:t + 1], a["L0_ffn_b1"][one, col:col + k].rearrange("o d -> d o")).then_inc(s.weights, 16)
                sp.wait_ge(s.m_res, GROUPS * l + GROUPS)
                hold(sp, s.held)

            with sp.Fori(0, GROUPS // 2) as m:
                for par in range(2):
                    sp.wait_ge(s.d_o, m * 2 + (par + 1))
                    sp.dma_start(out_rows[bass.ds(m * 8 + par * 4, 4), :, :].rearrange("t p d -> p t d"), OB[:, par, :, :]).then_inc(stored[par], 16)
            for par in range(2):
                sp.wait_ge(stored[par], 16 * GROUPS // 2)


        @block.tensor
        def _(pe):
            pe_state_space(pe)
            attention_layers(pe, pe_attention, pe_ffn, start=with_buffers)
            pe_linear(pe)
            pe_butterfly(pe)

        @block.scalar
        def _(act):
            act_state_space(act)
            attention_layers(act, act_attention, act_ffn, start=with_buffers)
            act_linear(act)
            act_butterfly(act)

        @block.vector
        def _(dve):
            dve_state_space(dve)
            attention_layers(dve, dve_attention, dve_ffn, start=with_buffers, each=dve_rope)
            dve_linear(dve)
            dve_butterfly(dve)

        @block.gpsimd
        def _(pool):
            pool_setup(pool)
            attention_layers(pool, pool_attention, pool_ffn, start=pool_start, each=pool_rope)
            pool_linear(pool)
            pool_butterfly(pool)


def kernel(**inputs):
    import numpy as _np
    import concourse.bacc as _bacc
    from concourse import mybir as _mybir
    from concourse.bass_utils import run_bass_kernel_spmd as _run

    nc = _bacc.Bacc("TRN2", target_bir_lowering=False, num_devices=1)
    arrays, aps = {}, {}
    for name, v in [*inputs.items(), *shape_constants().items()]:
        v = _np.ascontiguousarray(v)
        arrays[f"in_{name}"] = v
        aps[name] = nc.dram_tensor(f"in_{name}", v.shape, _mybir.dt.from_np(v.dtype), kind="ExternalInput").ap()
    out = nc.dram_tensor("out_x", (B, N, D), F32, kind="ExternalOutput").ap()
    build(nc, aps, out)
    r = _run(nc, [arrays], core_ids=[0])
    return r.results[0]["out_x"]
```

```python
from contextlib import ExitStack
from collections import namedtuple

import numpy as np
import concourse.bass as bass
from concourse import mybir

F32 = mybir.dt.float32
BF16 = mybir.dt.bfloat16
ALU = mybir.AluOpType
ACT = mybir.ActivationFunctionType
AX_X = mybir.AxisListType.X

P = 128
B, N, D = 4, 1024, 128
TOK = B * N
BANK = 512
EPS = 1e-5
ARENA = 25400

CH = 16
S = 16
CG = P // CH
G = D // CG
NCH = N // CH

DEPTH, HEADS, DH, WIN = 2, 8, 64, 64
INNER = HEADS * DH
PAIRS = HEADS // 2
TILES = TOK // P
TPB = N // P
HID = int(D * 4 * 2 / 3)
HT = [(j, min(P, HID - j)) for j in range(0, HID, P)]
PADN = N + 1
QK_SCALE = 8.0
SS_SCALE = 65536.0

HD1 = 8
HIDDEN = 512
STAGES = 9
LO_BITS = 4
LO, HI = 1 << LO_BITS, HIDDEN >> LO_BITS
GROUPS = TOK // BANK


def shape_constants():
    p = np.arange(P)
    half = np.arange(0, DH, 2, dtype=np.float32)
    inv = (np.float32(1.0) / np.float32(10000.0) ** (half / np.float32(DH))).astype(np.float32)
    t = np.arange(N, dtype=np.float32)
    fr = t[:, None] * inv[None, :]
    fr = np.concatenate([fr, fr], -1).astype(np.float64)
    base = (half + np.float32(0.4 * DH)) / np.float32(1.4 * DH)
    power = (t - N // 2) / np.float32(WIN // 2)
    sc = base[None, :].astype(np.float64) ** power[:, None].astype(np.float64)
    sc = np.concatenate([sc, sc], -1)
    cos, sin = np.cos(fr), np.sin(fr)
    sgn = np.where(np.arange(DH) < DH // 2, 1.0, -1.0)[None, :]
    rope = np.stack([cos * sc * QK_SCALE, cos / sc, sgn * sin * sc * QK_SCALE, sgn * sin / sc], 1)
    rope = rope * SS_SCALE ** 0.5
    rope = rope.reshape(TPB, P, 4 * DH).transpose(1, 0, 2)
    i = (p % WIN)[:, None]
    c = np.arange(WIN)[None, :]
    own = np.where(c <= i, 0.0, -1e38)
    before = np.where(c >= i, 0.0, -1e38)
    first = np.concatenate([own, np.full((P, WIN), -1e38)], 1)
    even = np.concatenate([own, before], 1)
    odd = np.concatenate([before, own], 1)
    masks = np.stack([first] + [even] * (TPB - 1) + [odd], 1)
    chan = p[:, None] // CH == np.arange(CG)[None, :]
    srow = np.zeros((P, P))
    srow[:S] = np.arange(S)[:, None] == p[None, :] % S
    powers = np.tile(np.arange(CH, -1, -1)[None, :], (P, 1))
    signs = np.where(powers % 2 == 0, 1.0, -1.0)
    shift = np.zeros((P, P + CH - 1))
    shift[p, CH - 1 + p // CH * CH] = 1.0
    anti = np.arange(CH)[None, :] == CH - 1 - (p % CH)[:, None]
    tables = {"rope": rope, "masks": masks, "ident": np.eye(P), "chan": chan, "srow": srow,
              "powers": powers, "signs": signs, "shift": shift, "anti": anti}
    return {k: np.ascontiguousarray(v, dtype=np.float32) for k, v in tables.items()}


SEMS = """
consts tables params x0 x1 att_weights ffn_weights l1_weights cweights
zeroed ones ct_ps ct_sb psel_ps psel_m abcd wbc powA expA es we e2w dg pre m2 m1_ps m1 upre_ps uw
negexp silu sil silrep modrep_ps modc_ps sel_ready clamp ln_nw
mods_ready modc_ready
ln_st ln_mv ln_ln ln_r ln_nb ln_x ln_m ln_h
hg_ps hg u_ps scan y_ps yg yt_ps y_t
t1_ps t1 t2_ps t2
wconl l1_cols hc_a ve_a g_hs_a buffers qk_ss rope_s
hc qk v tr sim pt pv ot wo_ps
qk_sq qk_ln qk_rn qkT v_sb ex ptT oT
qk_ssq qk_n qk_c qk_rot mx rinv on att_res
qk_s ve
g_hs g_tp g_st g_mv g_va g_r g_nb g_x g_tb g_h
m_gps m_g m_hid m_o m_res
c_cp c_qkv c_v c_max c_sub c_e c_sum c_rec c_qn c_kv c_kvp c_t0 c_t c_qt c_o c_x3 wt_ps wt
d_up d_g d_dn d_y d_x4 d_ot d_o
bu_t bu_y bd_t bd_y bias_w bb_t bb_y bb_sel bb_ps wc_ps wc wd_ps wd bcol
held qk_nw
""".split()
Signals = namedtuple("Signals", SEMS)


def build(nc, a, out):
    with ExitStack() as ctx:
        ctx.enter_context(nc.allow_non_contiguous_dma(reason="columns of small vectors"))
        def sb(name, *shape, dt=F32):
            return ctx.enter_context(nc.sbuf_tensor(name, [P, *shape], dt))

        s = Signals(*(ctx.enter_context(nc.semaphore("s_" + n)) for n in SEMS))
        bw = [ctx.enter_context(nc.semaphore(f"s_bw{n}")) for n in range(2)]
        stored = [ctx.enter_context(nc.semaphore(f"s_stored{n}")) for n in range(2)]

        def wait(eng, signal, value):
            if not isinstance(value, int) or value > 0:
                eng.wait_ge(signal, value)

        PS = ctx.enter_context(nc.psum_tensor("PS", [P, 8, BANK], F32))

        ident, identb = sb("ident", P), sb("identb", P, dt=BF16)
        ropec = sb("ropec", TPB, 4, DH)
        maskb = sb("maskb", TPB + 1, P, dt=BF16)
        chan, srow = sb("chan", CG), sb("srow", P)
        powers, signs = sb("powers", CH + 1), sb("signs", CH + 1)
        shift, anti = sb("shift", P + CH - 1), sb("anti", CH)
        ones, mhalf = sb("ones", P), sb("mhalf", 8)
        cT, wmod = sb("cT", 2, B), sb("wmod", 2, 6 * D)
        C_col = sb("C_col", S)
        wqkv, wo = sb("wqkv", 3 * INNER), sb("wo", PAIRS, D)
        w1, w2 = sb("w1", 2 * HID), sb("w2", len(HT), D)
        qks, b1c, lgc = sb("qks", 2, DH), sb("b1c", 2, len(HT)), sb("lgc", 3)
        ropes = sb("ropes", TPB, 4, DH)
        wq1, wqkvT = sb("wq1", 3, D), sb("wqkvT", 3 * D)
        wcon, bcol, bcols = sb("wcon", 4, D), sb("bcol", 5), sb("bcols", 6)
        b_hi, b_lo, b_sel = sb("b_hi", LO), sb("b_lo", HI), sb("b_sel", 4, CG)
        w_hi, w_lo, b_parts = sb("w_hi", LO_BITS, 2 * LO), sb("w_lo", STAGES - LO_BITS, HI // 2, 4), sb("b_parts", 2, HI)
        wu, wdT, wd = sb("wu", HIDDEN), sb("wdT", HIDDEN), sb("wd", 4, D)
        sil, silrep = sb("sil", 4, 2 * B), sb("silrep", 2, 2, P // 2)
        gar = sb("gar", 2, D)
        modc, gcol, gtmp = sb("modc", 2, 6, B), sb("gcol", 2, 2, B), sb("gtmp", 2, 4 * B)
        gtmr = sb("gtmr", 2, 2, D)

        XA, XB, X1 = sb("XA", B * PADN), sb("XB", B * PADN), sb("X1", TOK)
        arena = sb("arena", ARENA)

        def area(start, *shape, of=arena):
            names = "abcd"[:len(shape)]
            v = of[:, start:start + int(np.prod(shape))]
            if len(shape) > 1:
                v = v.rearrange(f"p ({' '.join(names)}) -> p {' '.join(names)}", **dict(zip(names[1:], shape[1:])))
            return v

        XP, HP = area(0, 2, CH, D), area(TOK, 2, D, CH)
        HG, HS = area(2 * TOK, G, 2 * P), area(3 * TOK, G, B, NCH + 1)
        YG, H2 = area(TOK, G, 2 * P), \
            area(2 * TOK, 2, CH, D)
        at = 4 * TOK + G * B
        UW, M1, M2 = area(at, G, P), area(at + G * P, G, P), area(at + 2 * G * P, G, P)
        upre = area(3 * TOK, G, CG, CH)
        A_row, B_row, D_row, C_row = (area(3 * PADN + 1 + n * D, D, of=XB) for n in range(4))
        bwr, cmp = area(0, 2, 4 * HIDDEN // 2, of=XB), area(2 * HIDDEN * 2, 2, HIDDEN, of=XB)
        maskf = area(at + 3 * G * P, TPB + 1, P)
        places, taken = [], 0
        for shape in ((4 * G, CG), (G, CH + 1), (G, CH + 1), (G, 2 * CH - 1), (G, CH), (G, CH), (2, CH, 32), (2, 3, D)):
            places.append(area(taken, *shape, of=X1))
            taken += int(np.prod(shape))
        assert taken <= TOK
        psel, ee, es, we, e2w, dg, ytmp, modr = places
        abcd, wbc, a16 = sb("abcd", 4, G), sb("wbc", G), sb("a16", G)
        stx, mvx, rsx = sb("stx", 2 * CH, 6), sb("mvx", 2 * CH, 2), sb("rsx", 3, 2 * CH)

        block = ctx.enter_context(nc.Block())

        out_rows = out.rearrange("b (t p) d -> (b t) p d", p=P)
        x_rows = a["L0_attn_x"].rearrange("b (k i) d -> (b k) (i d)", i=CH)

        N_CONST, N_PARAM, N_ATT, N_FFN = 16 * 7, 16 * 8, 16 * 4, 16 * 12

        def pe_state_space(pe):
            pe.wait_ge(s.consts, N_CONST)
            pe.wait_ge(s.params, N_PARAM)
            pe.transpose(PS[0:S, 0, 0:P], C_col[:, :], ident[:, :]).then_inc(s.ct_ps, 1)
            pe.wait_ge(s.sil, 1)
            for l in range(2):
                for j in range(6):
                    last = pe.matmul(PS[:, 1, (l * 6 + j) * B:(l * 6 + j + 1) * B], wmod[:, l, j * D:(j + 1) * D],
                                     sil[:, 3, l * B:(l + 1) * B], start=True, stop=True)
            last.then_inc(s.modc_ps, 1)
            pe.wait_ge(s.silrep, 1)
            for h in range(2):
                last = pe.matmul(PS[:, 2 + h, 0:3 * D], silrep[:, h, :, :], wmod[:, 0, 0:3 * D], start=True, stop=True)
            last.then_inc(s.modrep_ps, 1)
            pe.wait_ge(s.ct_sb, 1)
            pe.wait_ge(s.ones, 1)
            for j, (w, v) in enumerate(((srow[0:S, :], A_row[0:S, :]), (srow[0:S, :], B_row[0:S, :]),
                                        (srow[0:S, :], C_row[0:S, :]), (ones[0:1, :], D_row[0:1, :]))):
                last = pe.matmul(PS[:, 0, j * D:(j + 1) * D], w, v, start=True, stop=True)
            last.then_inc(s.psel_ps, 1)
            pe.wait_ge(s.we, 1)
            pe.wait_ge(s.dg, 1)
            pe.wait_ge(s.modrep_ps, 1)
            for j in range(CH):
                pe.matmul(PS[:, 4, 0:G * CH], shift[:, CH - 1 - j:CH - 1 - j + P], we[:, :, j:j + CH], start=(j == 0), stop=False)
            pe.matmul(PS[:, 4, 0:G * CH], ident[:, :], dg[:, :, :], start=False, stop=True).then_inc(s.m1_ps, 1)
            pe.wait_ge(s.wconl, 16)
            for j in range(4):
                t = pe.transpose(PS[:, 7, j * P:(j + 1) * P], wcon[:, j, :], ident[:, :])
            t.then_inc(s.wc_ps, 1)
            pe.wait_ge(s.pre, 1)
            pe.wait_ge(s.wc, 1)
            pe.wait_ge(s.mods_ready, 1)
            pe.wait_ge(s.modc_ready, 1)
            for g in range(G):
                if g == 12:
                    pe.wait_ge(s.m1, 1)
                if g == 4:
                    pe.wait_ge(s.psel_m, 1)
                t = pe.transpose(PS[:, (5, 6, 7, 4)[g // 4], (g % 4) * P:(g % 4 + 1) * P], upre[:, g, :, :], ident[:, :])
                if g % 4 == 3:
                    t.then_inc(s.upre_ps, 1)
            for k in range(8):
                if k == 0:
                    pe.wait_ge(s.ln_h, 2)
                    pe.wait_ge(s.uw, 4)
                for g in (2 * k, 2 * k + 1):
                    for h in range(2):
                        t = pe.transpose(PS[:, k, ((g % 2) * 2 + h) * P:((g % 2) * 2 + h + 1) * P],
                                         HP[:, h, CG * g:CG * g + CG, :], ident[:, :])
                t.then_inc(s.hg_ps, 1)
            for k in range(8):
                pe.wait_ge(s.hg, k + 1)
                for g in (2 * k, 2 * k + 1):
                    t = pe.matmul(PS[:, k, (g % 2) * 2 * P:(g % 2 + 1) * 2 * P], UW[:, g, :], HG[:, g, :], start=True, stop=True)
                t.then_inc(s.u_ps, 1)
            for k in range(8):
                pe.wait_ge(s.scan, k + 1)
                if k == 0:
                    pe.wait_ge(s.m1, 1)
                    pe.wait_ge(s.m2, 1)
                for g in (2 * k, 2 * k + 1):
                    o = PS[:, k, (g % 2) * 2 * P:(g % 2 + 1) * 2 * P]
                    pe.matmul(o, M1[:, g, :], HG[:, g, :], start=True, stop=False)
                    t = pe.matmul(o, M2[:, g, :], HS[:, g, :, 0:NCH], start=False, stop=True)
                t.then_inc(s.y_ps, 1)
            for k in range(8):
                q, h = k // 2, k % 2
                pe.wait_ge(s.yg, 2 * q + 2)
                for g in range(4 * q, 4 * q + 4):
                    t = pe.transpose(PS[:, k, (g % 4) * P:(g % 4 + 1) * P], YG[:, g, h * P:(h + 1) * P], ident[:, :])
                t.then_inc(s.yt_ps, 1)
            for src, ps, free, ready in ((XP, s.t1_ps, None, s.y_t), (H2, s.t2_ps, s.t1, None)):
                for k in range(8):
                    h, q = k // 4, k % 4
                    if ready is not None:
                        pe.wait_ge(ready, 8)
                    else:
                        if h == 1 and q >= 2:
                            pe.wait_ge(s.ln_h, 2 + CH // 2)
                        else:
                            pe.wait_ge(s.ln_x, 2 * CH + (CH + CH // 2 if h else CH))
                        pe.wait_ge(free, k + 1)
                    for i in range(4):
                        t = pe.transpose(PS[:, k, i * P:(i + 1) * P], src[:, h, 4 * q + i, :], ident[:, :])
                    t.then_inc(ps, 1)

        def butterfly_stage(eng, n, y, w, parts, transposed, st, t_done, y_done):
            w = w.rearrange("p (n q o i) -> p n q o i", q=st, o=2, i=2)
            halves = y[:, :].rearrange("p (n h q) -> p n h q", h=2, q=st)
            for h in range(2):
                part = (w[:, :, :, h, :] if transposed else w[:, :, :, :, h]).rearrange("p n q o -> p n o q")
                o = parts[:, h, :].rearrange("p (n h q) -> p n h q", h=2, q=st)
                for f in range(2):
                    eng.tensor_tensor(o[:, :, f, :], halves[:, :, h, :], part[:, :, f, :], ALU.mult).then_inc(t_done, 1)
            eng.wait_ge(t_done, 4 * (n + 1))
            eng.tensor_tensor(y[:, :], parts[:, 0, :], parts[:, 1, :], ALU.add).then_inc(y_done, 1)
            eng.wait_ge(y_done, n + 1)

        def second_input(k, b):
            h, q = k // 4, k % 4
            bb = 2 * h + b
            o = XA[:, bb * PADN + 1:(bb + 1) * PADN].rearrange("p (k i) -> p k i", i=CH)[:, :, 4 * q:4 * q + 4]
            return bb, o, PS[:, k, :].rearrange("p (i b k) -> p b k i", i=4, b=2)[:, b, :, :]

        def stage_weights(eng):
            n = 0
            for name, order in (("L1_ffn_up_weights", range(STAGES)), ("L1_ffn_down_weights", reversed(range(STAGES)))):
                for k in order:
                    if n >= 2:
                        eng.wait_ge(*((s.bu_y, n - 1) if n - 2 < STAGES else (s.bd_y, n - 1 - STAGES)))
                    eng.dma_start(bwr[:, n % 2, :], a[name][k:k + 1, :, :, :].rearrange("o w i j -> o (w i j)").to_broadcast([P, 2 * HIDDEN])).then_inc(bw[n % 2], 16)
                    n += 1

        def act_normalise(act, n, h, src, dst):
            r = slice(CH * h, CH * h + CH)
            act.wait_ge(s.ln_mv, 2 * n + h + 1)
            act.activation(rsx[:, 0, r], mvx[:, r, 1], ACT.Ln).then_inc(s.ln_ln, 1)
            act.wait_ge(s.ln_ln, 2 * n + h + 1)
            act.activation(rsx[:, 1, r], rsx[:, 0, r], ACT.Exp, scale=-0.5).then_inc(s.ln_r, 1)
            act.wait_ge(s.ln_nb, 2 * n + h + 1)
            for i in range(CH // 2 if (n, h) == (1, 1) else CH):
                act.activation(dst[:, h, :, i] if n == 0 else dst[:, h, i, :], src[:, h, i, :], ACT.Identity, bias=rsx[:, 2, CH * h + i:CH * h + i + 1],
                               scale=rsx[:, 1, CH * h + i:CH * h + i + 1]).then_inc(s.ln_x, 1)

        def act_state_space(act):
            act.preload_act_table_set("natural_log_exp_and_others")
            act_normalise(act, 0, 0, XP, HP)
            act.wait_ge(s.params, N_PARAM)
            act.activation(sil[:, 0, :], cT[:, :, :].rearrange("p l b -> p (l b)"), ACT.Exp, scale=-1.0).then_inc(s.negexp, 1)
            act_normalise(act, 0, 1, XP, HP)
            act.wait_ge(s.powA, 1)
            act.activation(es[:, :, :], ee[:, :, :], ACT.Exp).then_inc(s.expA, 1)
            act.wait_ge(s.wc_ps, 1)
            act.activation(wdT[:, :], PS[:, 7, :], ACT.Copy).then_inc(s.wc, 1)
            for k, bank in enumerate((5, 6, 7, 4)):
                act.wait_ge(s.upre_ps, k + 1)
                act.activation(UW[:, 4 * k:4 * k + 4, :], PS[:, bank, :].rearrange("p (g q) -> p g q", g=4), ACT.Copy).then_inc(s.uw, 1)
            for k in range(8):
                act.wait_ge(s.hg_ps, k + 1)
                act.activation(HG[:, 2 * k:2 * k + 2, :], PS[:, k, :].rearrange("p (g q) -> p g q", g=2), ACT.Copy).then_inc(s.hg, 1)
            for k in range(8):
                act.wait_ge(s.y_ps, k + 1)
                act.activation(YG[:, 2 * k:2 * k + 2, :], PS[:, k, :].rearrange("p (g q) -> p g q", g=2), ACT.Copy).then_inc(s.yg, 1)
            for k in range(8):
                h, q = k // 4, k % 4
                act.wait_ge(s.t1_ps, k + 1)
                o = X1[:, 2 * h * N:2 * (h + 1) * N].rearrange("p (b k i) -> p b k i", b=2, i=CH)[:, :, :, 4 * q:4 * q + 4]
                for b in range(2):
                    t = act.activation(o[:, b, :, :], PS[:, k, :].rearrange("p (i b k) -> p b k i", i=4, b=2)[:, b, :, :], ACT.Copy)
                t.then_inc(s.t1, 1)
            for h in range(2):
                act_normalise(act, 1, h, XP, H2)
            for k in range(4, 8):
                act.wait_ge(s.t2_ps, k + 1)
                for b in range(2):
                    bb, o, turned = second_input(k, b)
                    t = act.activation(o, turned, ACT.Identity, bias=modc[:, 0, 3, bb:bb + 1], scale=modc[:, 0, 4, bb:bb + 1])
                t.then_inc(s.t2, 1)

        def dve_refine(dve, n, r):
            dve.tensor_tensor(rsx[:, 2, r], rsx[:, 1, r], rsx[:, 1, r], ALU.mult).then_inc(s.ln_nw, 1)
            dve.wait_ge(s.ln_nw, 3 * n + 1)
            dve.scalar_tensor_tensor(rsx[:, 2, r], rsx[:, 2, r], -0.5, mvx[:, r, 1], ALU.mult, ALU.mult).then_inc(s.ln_nw, 1)
            dve.wait_ge(s.ln_nw, 3 * n + 2)
            dve.scalar_tensor_tensor(rsx[:, 1, r], rsx[:, 2, r], 1.5, rsx[:, 1, r], ALU.add, ALU.mult).then_inc(s.ln_nw, 1)
            dve.wait_ge(s.ln_nw, 3 * n + 3)
            dve.scalar_tensor_tensor(rsx[:, 2, r], mvx[:, r, 0], -1.0, rsx[:, 1, r], ALU.mult, ALU.mult).then_inc(s.ln_nb, 1)

        def dve_statistics(dve, n, h):
            for i in range(CH * h, CH * h + CH):
                t = dve.bn_stats(stx[:, i, :], XP[:, h, i - CH * h, :])
            t.then_inc(s.ln_st, 1)
            dve.wait_ge(s.ln_st, 2 * n + h + 1)
            for i in range(CH * h, CH * h + CH):
                t = dve.bn_aggr(mvx[:, i, :], stx[:, i, :])
            t.then_inc(s.ln_m, 1)
            r = slice(CH * h, CH * h + CH)
            dve.wait_ge(s.ln_m, 2 * n + h + 1)
            dve.tensor_scalar(mvx[:, r, 1], mvx[:, r, 1], EPS, None, ALU.add).then_inc(s.ln_mv, 1)
            dve.wait_ge(s.ln_r, 2 * n + h + 1)
            dve_refine(dve, 2 * n + h, r)

        def dve_clamp(dve, out_ap, g_ap, t0, t1):
            dve.tensor_scalar(t0, g_ap, 0.0, 2.0, ALU.is_ge, ALU.mult).then_inc(s.clamp, 1)
            dve.scalar_tensor_tensor(t1, g_ap, -1.0, g_ap, ALU.mult, ALU.max).then_inc(s.clamp, 1)
            dve.wait_ge(s.clamp, clamps[0] + 2)
            dve.tensor_scalar(t1, t1, 0.25, None, ALU.max).then_inc(s.clamp, 1)
            clamps[0] += 4
            dve.wait_ge(s.clamp, clamps[0] - 1)
            return dve.scalar_tensor_tensor(out_ap, t0, -1.0, t1, ALU.add, ALU.mult).then_inc(s.clamp, 1)

        clamps = [0]

        def dve_state_space(dve):
            for h, sx in enumerate((s.x0, s.x1)):
                dve.wait_ge(sx, 16)
                dve_statistics(dve, 0, h)
            dve.wait_ge(s.params, N_PARAM)
            dve.wait_ge(s.negexp, 1)
            dve.tensor_scalar(sil[:, 1, :], sil[:, 0, :], 1.0, None, ALU.add).then_inc(s.silu, 1)
            dve.wait_ge(s.silu, 1)
            dve.reciprocal(sil[:, 2, :], sil[:, 1, :]).then_inc(s.silu, 1)
            dve.wait_ge(s.silu, 2)
            dve.tensor_tensor(sil[:, 3, :], sil[:, 2, :], cT[:, :, :].rearrange("p l b -> p (l b)"), ALU.mult).then_inc(s.sil, 1)
            dve.wait_ge(s.sil, 1)
            dve.tensor_copy(silrep[:, :, :, :].rearrange("p h b k -> p (h b) k"),
                            sil[:, 3, 0:B].unsqueeze(2).to_broadcast([P, B, P // 2])).then_inc(s.silrep, 1)
            dve.wait_ge(s.ct_ps, 1)
            dve.tensor_copy(C_row[0:S, :], PS[0:S, 0, 0:P]).then_inc(s.ct_sb, 1)
            dve.wait_ge(s.psel_ps, 1)
            dve.tensor_tensor(psel[:, :, :], PS[:, 0, :].rearrange("p (a c) -> p a c", c=CG),
                              chan[:, :].unsqueeze(1).to_broadcast([P, 4 * G, CG]), ALU.mult).then_inc(s.psel_m, 1)
            dve.wait_ge(s.psel_m, 1)
            dve.tensor_reduce(abcd[:, :, :].rearrange("p a g -> p (a g)"), psel[:, :, :], AX_X, ALU.add).then_inc(s.abcd, 1)
            dve.wait_ge(s.abcd, 1)
            dve.tensor_tensor(ee[:, :, :], abcd[:, 0, :].unsqueeze(2).to_broadcast([P, G, CH + 1]),
                              powers[:, :].unsqueeze(1).to_broadcast([P, G, CH + 1]), ALU.mult).then_inc(s.powA, 1)
            dve.tensor_tensor(wbc[:, :], abcd[:, 1, :], abcd[:, 2, :], ALU.mult).then_inc(s.wbc, 1)
            dve.memset(we[:, :, :], 0.0).then_inc(s.zeroed, 1)
            dve.tensor_tensor(dg[:, :, :], abcd[:, 3, :].unsqueeze(2).to_broadcast([P, G, CH]),
                              anti[:, :].unsqueeze(1).to_broadcast([P, G, CH]), ALU.mult).then_inc(s.dg, 1)
            dve.wait_ge(s.expA, 1)
            dve.tensor_tensor(es[:, :, :], es[:, :, :], signs[:, :].unsqueeze(1).to_broadcast([P, G, CH + 1]), ALU.mult).then_inc(s.es, 1)
            dve.wait_ge(s.es, 1)
            dve.wait_ge(s.wbc, 1)
            dve.wait_ge(s.zeroed, 1)
            wide = wbc[:, :].unsqueeze(2).to_broadcast([P, G, CH])
            dve.tensor_tensor(we[:, :, 0:CH], es[:, :, 1:CH + 1], wide, ALU.mult).then_inc(s.we, 1)
            dve.tensor_tensor(e2w[:, :, :], es[:, :, 0:CH], wide, ALU.mult).then_inc(s.e2w, 1)
            dve.tensor_copy(a16[:, :], es[:, :, 0]).then_inc(s.e2w, 1)
            blocks = chan[:, :].unsqueeze(1).unsqueeze(3).to_broadcast([P, G, CG, CH])
            dve.tensor_tensor(upre, es[:, :, 1:CH + 1].unsqueeze(2).to_broadcast([P, G, CG, CH]), blocks, ALU.mult).then_inc(s.pre, 1)
            dve.wait_ge(s.modc_ps, 1)
            dve.tensor_copy(modc[:, :, :, :].rearrange("p l j b -> p (l j b)"), PS[:, 1, 0:48]).then_inc(s.sel_ready, 1)
            dve.wait_ge(s.sel_ready, 1)
            for l in range(2):
                for j in range(2):
                    dve_clamp(dve, gcol[:, l, j, :], modc[:, l, 2 + 3 * j, :], gtmp[:, 0, (2 * l + j) * B:(2 * l + j + 1) * B],
                              gtmp[:, 1, (2 * l + j) * B:(2 * l + j + 1) * B])
            for l in range(2):
                for j in (1, 4):
                    t = dve.tensor_scalar(modc[:, l, j, :], modc[:, l, j, :], 1.0, None, ALU.add)
            t.then_inc(s.modc_ready, 1)
            dve.wait_ge(s.modrep_ps, 1)
            for h in range(2):
                dve.tensor_copy(modr[:, h, 0:3, :].rearrange("p j d -> p (j d)"), PS[:, 2 + h, 0:3 * D]).then_inc(s.sel_ready, 1)
            dve.wait_ge(s.sel_ready, 3)
            for h in range(2):
                dve_clamp(dve, gar[:, h, :], modr[:, h, 2, :], gtmr[:, 0, h, :], gtmr[:, 1, h, :])
                t = dve.tensor_scalar(modr[:, h, 1, :], modr[:, h, 1, :], 1.0, None, ALU.add)
            t.then_inc(s.mods_ready, 1)
            dve.wait_ge(s.mods_ready, 1)
            for h in range(2):
                dve.wait_ge(s.ln_x, CH * (h + 1))
                dve.tensor_tensor(HP[:, h, :, :], HP[:, h, :, :], modr[:, h, 1, :].unsqueeze(2).to_broadcast([P, D, CH]), ALU.mult).then_inc(s.sel_ready, 1)
                dve.wait_ge(s.sel_ready, 4 + h)
                dve.tensor_tensor(HP[:, h, :, :], HP[:, h, :, :], modr[:, h, 0, :].unsqueeze(2).to_broadcast([P, D, CH]), ALU.add).then_inc(s.ln_h, 1)
            dve.wait_ge(s.e2w, 2)
            dve.tensor_tensor(M2[:, :, :].rearrange("p g (c i) -> p g c i", c=CG), e2w[:, :, :].unsqueeze(2).to_broadcast([P, G, CG, CH]),
                              blocks, ALU.mult).then_inc(s.m2, 1)
            dve.wait_ge(s.m1_ps, 1)
            dve.tensor_tensor(M1[:, :, :].rearrange("p g (c i) -> p g c i", c=CG),
                              PS[:, 4, 0:G * CH].rearrange("p (g i) -> p g i", g=G).unsqueeze(2).to_broadcast([P, G, CG, CH]),
                              blocks, ALU.mult).then_inc(s.m1, 1)
            dve.wait_ge(s.upre_ps, 4)
            dve.memset(HS[:, :, :, 0], 0.0).then_inc(s.zeroed, 1)
            for k in range(8):
                dve.wait_ge(s.u_ps, k + 1)
                for g in (2 * k, 2 * k + 1):
                    for b in range(B):
                        c0 = (g % 2) * 2 * P + b * NCH
                        t = dve.tensor_tensor_scan(HS[:, g, b, 1:NCH + 1], a16[:, g:g + 1].to_broadcast([P, NCH]),
                                                   PS[:, k, c0:c0 + NCH], 0.0, ALU.mult, ALU.add)
                t.then_inc(s.scan, 1)
            for k in range(8):
                q, h = k // 2, k % 2
                dve.wait_ge(s.yt_ps, k + 1)
                y = PS[:, k, :].rearrange("p (gc i) -> p i gc", i=CH)[:, ::-1, :]
                c = slice(32 * q, 32 * q + 32)
                dve.tensor_tensor(ytmp[:, k % 2, :, :], y, gar[:, h, c].unsqueeze(1).to_broadcast([P, CH, 32]), ALU.mult).then_inc(s.ln_m, 1)
                dve.wait_ge(s.ln_m, 2 + k + 1)
                dve.tensor_tensor(XP[:, h, :, c], XP[:, h, :, c], ytmp[:, k % 2, :, :], ALU.add).then_inc(s.y_t, 1)
            dve.wait_ge(s.y_t, 8)
            ln_m_base = 8
            for h in range(2):
                for i in range(CH * h, CH * h + CH):
                    t = dve.bn_stats(stx[:, i, :], XP[:, h, i - CH * h, :])
                t.then_inc(s.ln_st, 1)
                dve.wait_ge(s.ln_st, 2 + h + 1)
                for i in range(CH * h, CH * h + CH):
                    t = dve.bn_aggr(mvx[:, i, :], stx[:, i, :])
                t.then_inc(s.ln_m, 1)
                r = slice(CH * h, CH * h + CH)
                dve.wait_ge(s.ln_m, 2 + ln_m_base + h + 1)
                dve.tensor_scalar(mvx[:, r, 1], mvx[:, r, 1], EPS, None, ALU.add).then_inc(s.ln_mv, 1)
                dve.wait_ge(s.ln_r, 2 + h + 1)
                dve_refine(dve, 2 + h, r)
            dve.wait_ge(s.ln_nb, 4)
            for i in range(CH // 2, CH):
                dve.tensor_scalar(H2[:, 1, i, :], XP[:, 1, i, :], rsx[:, 1, CH + i:CH + i + 1], rsx[:, 2, CH + i:CH + i + 1],
                                  ALU.mult, ALU.add).then_inc(s.ln_h, 1)
            for k in range(4):
                dve.wait_ge(s.t2_ps, k + 1)
                for b in range(2):
                    bb, o, turned = second_input(k, b)
                    t = dve.tensor_scalar(o, turned, modc[:, 0, 4, bb:bb + 1], modc[:, 0, 3, bb:bb + 1], ALU.mult, ALU.add)
                t.then_inc(s.t2, 1)
            dve.wait_ge(s.bias_w, 16 * (1 + STAGES))
            for k in range(LO_BITS):
                butterfly_stage(dve, k, b_hi[0:HI], w_hi[0:HI, k, :], b_parts[0:HI, :, 0:LO], False, 1 << k, s.bb_t, s.bb_y)

        def dve_bias(dve):
            dve.wait_ge(s.bb_ps, 1)
            dve.tensor_copy(b_lo[0:LO, :], PS[0:LO, 4, 0:HI]).then_inc(s.bb_sel, 1)
            dve.wait_ge(s.bb_sel, 1)
            for k in range(LO_BITS, STAGES):
                butterfly_stage(dve, k, b_lo[0:LO], w_lo[0:LO, k - LO_BITS, :, :].rearrange("l g c -> l (g c)"), b_parts[0:LO, :, :], False,
                                1 << (k - LO_BITS), s.bb_t, s.bb_y)

        def pool_setup(pool):
            pool.memset(ones[:, :], 1.0).then_inc(s.ones, 1)
            pool.memset(mhalf[:, :], -0.5).then_inc(s.ones, 1)
            pool_compose(pool)
            pool.wait_ge(s.consts, N_CONST)
            pool.wait_ge(s.tables, 16 * 2)
            pool.tensor_copy(identb[:, :], ident[:, :]).then_inc(s.buffers, 1)
            pool.tensor_copy(maskb[:, :, :], maskf[:, :, :]).then_inc(s.buffers, 1)
            for t in (XA, XB):
                pool.memset(t[:, :].rearrange("p (b t) -> p b t", b=B)[:, :, 0], 0.0).then_inc(s.buffers, 1)

        class Cut:
            def __init__(self, start=0):
                self.at = start

            def __call__(self, *shape):
                v = area(self.at, *shape)
                self.at += int(np.prod(shape))
                assert self.at <= ARENA
                return v

        cut = Cut()
        HC = cut(2, P)
        SQ, QN, QC, QS = (cut(2, HEADS, DH) for _ in range(4))
        assert cut.at >= TOK
        QH = cut(2, PAIRS, P)
        KT = cut(2, PAIRS, 3, WIN)
        assert cut.at <= 2 * TOK
        QR = cut(2, HEADS, DH)
        cut(PAIRS * 2 * P)
        EX = cut(2, 2 * PAIRS, P)
        PTs = cut(2 * PAIRS, P)
        VE = cut(2, HEADS, DH + 1)
        assert cut.at >= 3 * TOK
        VO = cut(2, HEADS, DH + 1)
        ON, OT = cut(HEADS, DH), cut(2, PAIRS, P)
        nrm = sb("nrm", 4, 2 * HEADS)
        mxs, rin = sb("mxs", 2 * PAIRS), sb("rin", HEADS)
        HSG_AT = cut.at
        HSG, HNG, HFG = cut(2, BANK), cut(4, P), cut(2, BANK)
        GE, HD = cut(2, BANK), cut(len(HT), BANK)
        stg, mvg, rsg, nbg = sb("stg", 4, 6), sb("mvg", 4, 2), sb("rsg", 4), sb("nbg", 4)

        def batch(t, bits):
            b = t >> bits
            return b if isinstance(b, int) else b.with_bounds(max_val=B - 1)

        def tok(t):
            return t * P + batch(t, 3) + 1

        def gtok(m):
            return m * BANK + batch(m, 1) + 1

        def cols(start, n):
            return slice(start, start + n) if isinstance(start, int) else bass.ds(start, n)

        def within(eng, signal, base, k, most=None):
            if isinstance(k, int):
                k = k if most is None else min(k, most)
                if k <= 0:
                    return
            eng.wait_ge(signal, base + k)

        def hold(eng, signal):
            eng.sem_inc(signal, 1)

        def pipeline(eng, steps, last, stages, first_pair, pairs):
            def step(n, parity, inside):
                for lag, f in stages:
                    if inside or 0 <= n - lag < steps:
                        f(n - lag, (parity - lag) % 2)
            for n in range(-1, first_pair):
                step(n, n % 2, False)
            hold(eng, s.held)
            with eng.Fori(0, pairs) as q:
                for k in range(2):
                    step(q * 2 + (first_pair + k), (first_pair + k) % 2, True)
            for n in range(first_pair + 2 * pairs, last):
                step(n, n % 2, False)

        def pe_attention(pe, L):
            def qk(t, par):
                within(pe, s.hc, L, t + 1)
                within(pe, s.qk_n, L, t)
                pe.matmul(PS[:, 0, :], HC[:, par, :], wqkv[:, 0:INNER], start=True, stop=True)
                pe.matmul(PS[:, 1, :], HC[:, par, :], wqkv[:, INNER:2 * INNER], start=True, stop=True).then_inc(s.qk, 1)

            def v(t, par):
                within(pe, s.v_sb, L, t)
                within(pe, s.oT, L, t - 1)
                pe.matmul(PS[:, 6, :], HC[:, par, :], wqkv[:, 2 * INNER:3 * INNER], start=True, stop=True).then_inc(s.v, 1)

            def turn_qk(t, par):
                within(pe, s.qk_rot, L, t + 1)
                within(pe, s.ptT, L, t - 1)
                for j in range(2):
                    for hp in range(PAIRS):
                        x = pe.transpose(PS[:, 2 + j, hp * P:(hp + 1) * P], QR[:, j, 2 * hp:2 * hp + 2, :], ident[:, :])
                x.then_inc(s.tr, 1)

            def scores(t, par):
                within(pe, s.qkT, L, t + 1)
                within(pe, s.ex, L, t)
                for w in range(2):
                    m = maskb[:, cols(t & 7, 1), :] if w == 0 else maskb[:, TPB:TPB + 1, :]
                    pe.matmul(PS[:, 4 + w, :], identb[:, :], m.to_broadcast([P, PAIRS, P]), start=True, stop=False, skip_group_check=True)
                for w in range(2):
                    for hp in range(PAIRS):
                        for e in range(2):
                            rows, o = slice(DH * e, DH * e + DH), WIN * (e ^ w)
                            k = KT[rows, par, hp, 0:2, :] if w == 0 else KT[rows, par, hp, 0:3:2, :]
                            x = pe.matmul(PS[o:o + WIN, 4 + w, hp * P:(hp + 1) * P], QH[rows, par, hp, w * WIN:w * WIN + WIN], k,
                                          start=False, stop=(hp == PAIRS - 1), skip_group_check=True)
                x.then_inc(s.sim, 1)

            def turn_p(t, par):
                within(pe, s.ex, L, t + 1)
                within(pe, s.qkT, L, t + 2, TILES)
                for k in range(2 * PAIRS):
                    x = pe.transpose(PS[:, 2 + k // PAIRS, (k % PAIRS) * P:(k % PAIRS + 1) * P], EX[:, par, k, :], ident[:, :])
                x.then_inc(s.pt, 1)

            def pv(t, par):
                within(pe, s.ptT, L, t + 1)
                within(pe, s.ve, L, t + 1)
                within(pe, s.v_sb, L, t + 2, TILES)
                within(pe, s.att_res, L, t)
                for h in range(HEADS):
                    for w in range(2):
                        x = pe.matmul(PS[WIN * w:WIN * w + WIN, 6 + h // 4, (h % 4) * (DH + 1):(h % 4 + 1) * (DH + 1)],
                                      PTs[:, w * PAIRS + h // 2, (h % 2 ^ w) * WIN:(h % 2 ^ w) * WIN + WIN],
                                      (VE, VO)[w][:, par, h, :], start=True, stop=True)
                x.then_inc(s.pv, 1)

            def turn_o(t, par):
                within(pe, s.on, L, t + 1)
                for hp in range(PAIRS):
                    x = pe.transpose(PS[:, 6, hp * P:(hp + 1) * P], ON[:, 2 * hp:2 * hp + 2, :], ident[:, :])
                x.then_inc(s.ot, 1)

            def project(t, par):
                within(pe, s.oT, L, t + 1)
                for hp in range(PAIRS):
                    x = pe.matmul(PS[:, 7, 0:P], wo[:, hp, :], OT[:, par, hp, :], start=(hp == 0), stop=(hp == PAIRS - 1))
                x.then_inc(s.wo_ps, 1)

            pipeline(pe, TILES, TILES + 3, ((0, qk), (3, turn_o), (1, turn_qk), (3, project), (1, v), (2, turn_p), (1, scores), (2, pv)), 5, 12)

        def act_attention(act, L):
            def turned_q(t, par):
                within(act, s.tr, L, t + 1)
                within(act, s.sim, L, t)
                act.activation(QH[:, par, :, :], PS[:, 2, :].rearrange("p (h q) -> p h q", h=PAIRS), ACT.Copy)

            def turned_k(t, par):
                kt = PS[:, 3, :].rearrange("p (h w q) -> p h w q", h=PAIRS, w=2)
                act.activation(KT[:, par, :, 0:3:2, :], kt, ACT.Copy)
                act.activation(KT[:, 1 - par, :, 1, :], kt[:, :, 1, :], ACT.Copy).then_inc(s.qkT, 1)

            def values(t, par):
                within(act, s.v, L, t + 1)
                within(act, s.pv, L, t - 1)
                within(act, s.ve, L, t)
                act.activation(VO[:, par, :, 0:DH], PS[:, 6, :].rearrange("p (h d) -> p h d", h=HEADS), ACT.Copy).then_inc(s.v_sb, 1)

            def squares(t, par):
                within(act, s.qk, L, t + 1)
                within(act, s.qk_ssq, L, t)
                act.activation(SQ, PS[:, 0:2, :].rearrange("p j (h d) -> p j h d", h=HEADS), ACT.Square).then_inc(s.qk_sq, 1)

            def rnorm(t, par):
                within(act, s.qk_ssq, L, t + 1)
                act.activation(nrm[:, 1, :], nrm[:, 0, :], ACT.Ln, scale=SS_SCALE).then_inc(s.qk_ln, 1)
                within(act, s.qk_ln, L, t + 1)
                within(act, s.qk_n, L, t)
                act.activation(nrm[:, 2, :], nrm[:, 1, :], ACT.Exp, scale=-0.5).then_inc(s.qk_rn, 1)

            def turned_p(t, par):
                within(act, s.pt, L, t + 1)
                within(act, s.pv, L, t)
                act.activation(PTs, PS[:, 2:4, :].rearrange("p w (h q) -> p (w h) q", h=PAIRS), ACT.Copy).then_inc(s.ptT, 1)

            def exponentials(t, par):
                within(act, s.mx, L, t + 1)
                within(act, s.pt, L, t - 1)
                for k in range(2 * PAIRS):
                    x = act.activation(EX[:, par, k, :], PS[:, 4 + k // PAIRS, (k % PAIRS) * P:(k % PAIRS + 1) * P], ACT.Exp, bias=mxs[:, k:k + 1])
                x.then_inc(s.ex, 1)

            hold(act, s.held)
            act.preload_act_table_set("natural_log_exp_and_others")
            pipeline(act, TILES, TILES + 3, ((0, squares), (1, turned_q), (1, turned_k), (0, rnorm), (1, values), (2, turned_p), (1, exponentials)), 5, 12)

        def dve_attention(dve, L):
            def outputs(t, par):
                within(dve, s.pv, L, t + 1)
                o = PS[:, 6:8, 0:4 * (DH + 1)].rearrange("p b (h e) -> p b h e", h=4)
                dve.reciprocal(rin[:, :].rearrange("p (b h) -> p b h", b=2), o[:, :, :, DH]).then_inc(s.rinv, 1)
                within(dve, s.rinv, L, t + 1)
                within(dve, s.ot, L, t)
                dve.tensor_tensor(ON.rearrange("p (b h) d -> p b h d", b=2), o[:, :, :, 0:DH],
                                  rin[:, :].rearrange("p (b h) -> p b h", b=2).unsqueeze(3).to_broadcast([P, 2, 4, DH]), ALU.mult).then_inc(s.on, 1)

            def turned_o(t, par):
                within(dve, s.ot, L, t + 1)
                within(dve, s.wo_ps, L, t - 1)
                dve.tensor_copy(OT[:, par, :, :], PS[:, 6, :].rearrange("p (h q) -> p h q", h=PAIRS)).then_inc(s.oT, 1)

            def norms(t, par):
                within(dve, s.qk_sq, L, t + 1)
                within(dve, s.qk_ln, L, t)
                dve.tensor_reduce(nrm[:, 0, :], SQ.rearrange("p j h d -> p (j h) d"), AX_X, ALU.add).then_inc(s.qk_ss, 1)
                within(dve, s.qk_ss, L, t + 1)
                dve.tensor_scalar(nrm[:, 0, :], nrm[:, 0, :], 1e-24, None, ALU.max).then_inc(s.qk_ssq, 1)

            def normed(t, par):
                within(dve, s.qk_rn, L, t + 1)
                dve.tensor_tensor(nrm[:, 3, :], nrm[:, 2, :], nrm[:, 2, :], ALU.mult).then_inc(s.qk_nw, 1)
                within(dve, s.qk_nw, 3 * L, 3 * t + 1)
                dve.scalar_tensor_tensor(nrm[:, 3, :], nrm[:, 3, :], -0.5 * SS_SCALE, nrm[:, 0, :], ALU.mult, ALU.mult).then_inc(s.qk_nw, 1)
                within(dve, s.qk_nw, 3 * L, 3 * t + 2)
                dve.scalar_tensor_tensor(nrm[:, 3, :], nrm[:, 3, :], 1.5, nrm[:, 2, :], ALU.add, ALU.mult).then_inc(s.qk_nw, 1)
                within(dve, s.qk_nw, 3 * L, 3 * t + 3)
                within(dve, s.qk_s, L, t)
                within(dve, s.qk_c, L, t)
                dve.tensor_tensor(QN.rearrange("p j h d -> p (j h) d"), PS[:, 0:2, :].rearrange("p j (h d) -> p (j h) d", h=HEADS),
                                  nrm[:, 3, :].unsqueeze(2).to_broadcast([P, 2 * HEADS, DH]), ALU.mult).then_inc(s.qk_n, 1)

            def cosines(t, par):
                within(dve, s.qk_n, L, t + 1)
                within(dve, s.qk_rot, L, t)
                tab = ropes[:, cols(t & 7, 1), 0:2, :].rearrange("p t j d -> p (t j) d").unsqueeze(2).to_broadcast([P, 2, HEADS, DH])
                dve.tensor_tensor(QC, QN, tab, ALU.mult).then_inc(s.qk_c, 1)

            def rotated(t, par):
                within(dve, s.qk_s, L, t + 1)
                within(dve, s.qk_c, L, t + 1)
                within(dve, s.tr, L, t)
                halves = "p j h (x d) -> p (j h) x d"
                dve.tensor_tensor(QR.rearrange(halves, x=2), QC.rearrange(halves, x=2),
                                  QS.rearrange(halves, x=2)[:, :, ::-1, :], ALU.add).then_inc(s.qk_rot, 1)

            def residual(t, par):
                within(dve, s.wo_ps, L, t + 1)
                c = cols(tok(t), P)
                dve.tensor_tensor(XB[:, c], PS[:, 7, 0:P], XA[:, c], ALU.add).then_inc(s.att_res, 1)

            def maxima(t, par):
                within(dve, s.sim, L, t + 1)
                within(dve, s.ex, L, t)
                sc = PS[:, 4:6, :].rearrange("p w (h k) -> p (w h) k", h=PAIRS)
                dve.tensor_reduce(mxs[:, :], sc, AX_X, ALU.max, negate=True).then_inc(s.mx, 1)

            pipeline(dve, TILES, TILES + 3, ((3, outputs), (1, rotated), (3, turned_o), (0, norms), (3, residual), (0, normed), (0, cosines), (1, maxima)), 5, 12)

        def pool_attention(pool, L):
            def shifted(t, par):
                within(pool, s.v, L, t - 1)
                hold(pool, s.held)
                pool.tensor_copy(HC[0:64, par, :], XA[0:64, cols(tok(t), P)]).then_inc(s.hc_a, 1)
                within(pool, s.hc_a, L, t + 1)
                hold(pool, s.held)
                pool.tensor_copy(HC[64:128, par, :], XA[64:128, cols(tok(t) - 1, P)]).then_inc(s.hc, 1)
                within(pool, s.hc, L, t + 1)

            def even_values(t, par):
                within(pool, s.v_sb, L, t + 1)
                within(pool, s.pv, L, t - 1)
                hold(pool, s.held)
                pool.tensor_copy(VE[0:64, par, :, :], VO[0:64, par, :, :]).then_inc(s.ve_a, 1)
                within(pool, s.ve_a, L, t + 1)
                hold(pool, s.held)
                pool.tensor_copy(VE[64:128, par, :, :], VO[64:128, 1 - par, :, :]).then_inc(s.ve, 1)
                within(pool, s.ve, L, t + 1)

            def sines(t, par):
                within(pool, s.qk_n, L, t + 1)
                within(pool, s.qk_rot, L, t)
                tab = ropes[:, cols(t & 7, 1), 2:4, :].rearrange("p t j d -> p (t j) d").unsqueeze(2).to_broadcast([P, 2, HEADS, DH])
                pool.tensor_tensor(QS, QN, tab, ALU.mult).then_inc(s.qk_s, 1)

            pipeline(pool, TILES, TILES + 3, ((-1, shifted), (0, sines), (1, even_values)), 5, 12)

        def pe_turn(pe, base, m, par):
            within(pe, s.g_hs, base, m + 1)
            within(pe, s.g_x, base, m)
            for i in range(4):
                x = pe.transpose(PS[:, 5, i * P:(i + 1) * P], HSG[:, par, i * P:(i + 1) * P], ident[:, :])
            x.then_inc(s.g_tp, 1)

        def pe_turn_back(pe, base, m, par):
            within(pe, s.g_x, base, m + 1)
            within(pe, s.g_h, base, m)
            for i in range(4):
                x = pe.transpose(PS[:, 6, i * P:(i + 1) * P], HNG[:, i, :], ident[:, :])
            x.then_inc(s.g_tb, 1)

        def dve_stats(dve, base, m, par):
            within(dve, s.g_tp, base, m + 1)
            for i in range(4):
                x = dve.bn_stats(stg[:, i, :], PS[:, 5, i * P:(i + 1) * P])
            x.then_inc(s.g_st, 1)
            within(dve, s.g_st, base, m + 1)
            within(dve, s.g_x, base, m)
            hold(dve, s.held)
            for i in range(4):
                x = dve.bn_aggr(mvg[:, i, :], stg[:, i, :])
            x.then_inc(s.g_mv, 1)
            within(dve, s.g_mv, base, m + 1)
            dve.tensor_scalar(mvg[:, :, 1], mvg[:, :, 1], EPS, None, ALU.add).then_inc(s.g_va, 1)

        def pool_rstd(pool, base, m, par):
            within(pool, s.g_va, base, m + 1)
            pool.tensor_tensor(rsg[:, :], mvg[:, :, 1], mhalf[:, 0:4], ALU.pow).then_inc(s.g_r, 1)

        def dve_center(dve, base, m, par):
            within(dve, s.g_r, base, m + 1)
            within(dve, s.g_tb, base, m)
            for i in range(4):
                x = dve.tensor_scalar(HNG[:, i, :], PS[:, 5, i * P:(i + 1) * P], mvg[:, i, 0:1], rsg[:, i:i + 1], ALU.subtract, ALU.mult)
            x.then_inc(s.g_x, 1)

        NH = len(HT)

        def pe_ffn(pe, base):
            def up(j):
                def f(m, par):
                    row, k = HT[j]
                    if j == 0:
                        within(pe, s.g_h, base, m + 1)
                    pr = 2 * ((NH * par + j) % 2)
                    within(pe, s.m_hid, base * NH, m * NH + j - 1)
                    pe.matmul(PS[0:k, pr, :], w1[:, row:row + k], HFG[:, par, :], start=True, stop=True)
                    pe.matmul(PS[0:k, pr + 1, :], w1[:, HID + row:HID + row + k], HFG[:, par, :], start=True, stop=True).then_inc(s.m_gps, 1)
                return f

            def down(m, par):
                within(pe, s.m_hid, base * NH, m * NH + NH)
                within(pe, s.m_res, base, m)
                for j, (row, k) in enumerate(HT):
                    x = pe.matmul(PS[:, 4, :], w2[0:k, j, :], HD[0:k, j, :], start=(j == 0), stop=(j == NH - 1))
                x.then_inc(s.m_o, 1)

            pipeline(pe, GROUPS, GROUPS + 2, ((1, up(0)), (2, down), (1, up(1)), (0, lambda m, p: pe_turn_back(pe, base, m, p)), (1, up(2)),
                                              (-1, lambda m, p: pe_turn(pe, base, m, p))), 3, 2)

        def act_ffn(act, base):
            def gelu(j):
                def f(m, par):
                    k, x = HT[j][1], (NH * par + j) % 2
                    within(act, s.m_gps, base * NH, m * NH + j + 1)
                    within(act, s.m_hid, base * NH, m * NH + j - 1)
                    act.activation(GE[0:k, x, :], PS[0:k, 2 * x + 1, :], ACT.Gelu, bias=b1c[0:k, 1, j:j + 1]).then_inc(s.m_g, 1)
                return f

            def scaled(m, par):
                within(act, s.g_tb, base, m + 1)
                within(act, s.m_o, base, m - 1)
                act.activation(HFG[:, par, :], PS[:, 6, :], ACT.Identity, bias=lgc[:, 1:2], scale=lgc[:, 0:1]).then_inc(s.g_h, 1)

            pipeline(act, GROUPS, GROUPS + 1, ((1, gelu(0)), (1, gelu(1)), (0, scaled), (1, gelu(2))), 3, 2)

        def dve_ffn(dve, base):
            def hidden(j):
                def f(m, par):
                    k = HT[j][1]
                    x = (NH * par + j) % 2
                    within(dve, s.m_g, base * NH, m * NH + j + 1)
                    within(dve, s.m_o, base, m)
                    dve.scalar_tensor_tensor(HD[0:k, j, :], PS[0:k, 2 * x, :], b1c[0:k, 0, j:j + 1], GE[0:k, x, :], ALU.add, ALU.mult).then_inc(s.m_hid, 1)
                return f

            def residual(m, par):
                within(dve, s.m_o, base, m + 1)
                c = cols(gtok(m), BANK)
                dve.scalar_tensor_tensor(XA[:, c], PS[:, 4, :], lgc[:, 2:3], XB[:, c], ALU.add, ALU.add).then_inc(s.m_res, 1)

            pipeline(dve, GROUPS, GROUPS + 2, ((0, lambda m, p: dve_stats(dve, base, m, p)), (0, lambda m, p: dve_center(dve, base, m, p)), (2, residual),
                                               (1, hidden(0)), (1, hidden(1)), (1, hidden(2))), 3, 2)

        def pool_ffn(pool, base):
            def shifted(m, par):
                within(pool, s.g_tp, base, m - 1)
                hold(pool, s.held)
                pool.tensor_copy(HSG[0:64, par, :], XB[0:64, cols(gtok(m), BANK)]).then_inc(s.g_hs_a, 1)
                within(pool, s.g_hs_a, base, m + 1)
                hold(pool, s.held)
                pool.tensor_copy(HSG[64:128, par, :], XB[64:128, cols(gtok(m) - 1, BANK)]).then_inc(s.g_hs, 1)
                within(pool, s.g_hs, base, m + 1)

            pipeline(pool, GROUPS, GROUPS + 1, ((0, lambda m, p: pool_rstd(pool, base, m, p)), (-1, shifted)), 3, 2)

        def nothing(*_):
            pass

        def attention_layers(eng, attention, ffn, each=nothing):
            eng.wait_ge(s.t2, 8)
            with_buffers(eng)
            with eng.Fori(0, DEPTH) as l:
                eng.wait_ge(s.att_weights, l * N_ATT + N_ATT)
                each(eng, l)
                attention(eng, l * TILES)
                eng.wait_ge(s.att_res, l * TILES + TILES)
                eng.wait_ge(s.ffn_weights, l * N_FFN + N_FFN)
                ffn(eng, l * GROUPS)
                eng.wait_ge(s.m_res, l * GROUPS + GROUPS)
                hold(eng, s.held)

        def dve_rope(dve, l):
            dve.wait_ge(s.tables, 16 * 2)
            dve.tensor_tensor(ropes[:, :, :, :].rearrange("p t (x j) d -> p (t x) (j d)", x=2),
                              ropec[:, :, :, :].rearrange("p t (x j) d -> p (t x) (j d)", x=2),
                              qks[:, :, :].rearrange("p j d -> p (j d)").unsqueeze(1).to_broadcast([P, 2 * TPB, 2 * DH]), ALU.mult).then_inc(s.rope_s, 1)
            dve.wait_ge(s.rope_s, l + 1)

        def pool_start(pool):
            pool.wait_ge(s.y_ps, 8)
            pool.wait_ge(s.yt_ps, 8)
            pool.memset(KT, 0.0).then_inc(s.buffers, 1)
            pool.memset(VO, 0.0).then_inc(s.buffers, 1)
            pool.wait_ge(s.buffers, 6)
            pool.memset(VO[:, :, :, DH], 1.0).then_inc(s.buffers, 1)

        def with_buffers(eng):
            eng.wait_ge(s.buffers, 7)
            eng.wait_ge(s.ones, 2)

        def pe_start(pe):
            pe.wait_ge(s.bb_y, LO_BITS)
            pe.wait_ge(s.t2, 8)
            pe.transpose(PS[0:LO, 4, 0:HI], b_hi[0:HI, :], ident[0:HI, 0:HI]).then_inc(s.bb_ps, 1)
            pe.wait_ge(s.bb_sel, 1)


        H1 = D // HD1
        cut4 = Cut()
        QKE, VT = cut4(2, 4, 2 * D), cut4(2, 4, D)
        KV, KVs = cut4(4, H1, HD1 * HD1), cut4(2, HD1 * HD1)
        TT, QT = cut4(4, HD1 * HD1), cut4(4, HD1, D)
        MX, ZS, ZI = cut4(4, H1 + HD1), cut4(4, H1 + HD1), cut4(4, H1 + HD1)
        assert cut4.at <= HSG_AT
        Q0 = DEPTH * GROUPS

        def key_value(eng, par, i, done):
            eng.tensor_tensor(KV[:, i, :, :].rearrange("p h (d e) -> p h d e", e=HD1),
                              QKE[:, par, i, D:].rearrange("p (h d) -> p h d", d=HD1).unsqueeze(3).to_broadcast([P, H1, HD1, HD1]),
                              VT[:, par, i, :].rearrange("p (h e) -> p h e", e=HD1).unsqueeze(2).to_broadcast([P, H1, HD1, HD1]),
                              ALU.mult).then_inc(done, 1)

        def by_softmax(v):
            return v[:, :, 0:D].rearrange("p i (h d) -> p i h d", d=HD1), v[:, :, D:].rearrange("p i (h d) -> p i d h", d=HD1)

        def spread(v):
            return v[:, :, 0:H1].unsqueeze(3).to_broadcast([P, 4, H1, HD1]), v[:, :, H1:].unsqueeze(3).to_broadcast([P, 4, HD1, H1])

        def pe_linear(pe):
            pe.wait_ge(s.l1_weights, 16 * 3)
            pe.wait_ge(s.m_res, DEPTH * GROUPS)
            for j in range(3):
                x = pe.transpose(PS[:, 0, j * P:(j + 1) * P], wq1[:, j, :], ident[:, :])
            x.then_inc(s.wt_ps, 1)
            pe.wait_ge(s.wt, 1)

            def qkv(m, par):
                within(pe, s.g_h, Q0, m + 1)
                within(pe, s.c_sub, 0, m * 2)
                within(pe, s.c_v, 0, m)
                for i in range(4):
                    x = pe.matmul(PS[:, i, 0:3 * D], HFG[:, par, i * P:(i + 1) * P], wqkvT[:, :], start=True, stop=True)
                x.then_inc(s.c_qkv, 1)

            def summed(i):
                def f(m, par):
                    within(pe, s.c_x3, 0, m)
                    within(pe, s.c_qt, 0, m * 4 + (i + 1))
                    for d in range(HD1):
                        x = pe.matmul(PS[:, 4, i * P:(i + 1) * P], QT[:, i, d, :], ident[:, :], start=(d == 0), stop=(d == HD1 - 1))
                    x.then_inc(s.c_o, 1)
                return f

            pipeline(pe, GROUPS, GROUPS + 1, ((0, lambda m, p: pe_turn_back(pe, Q0, m, p)), (0, qkv), (1, summed(0)), (1, summed(1)), (-1, lambda m, p: pe_turn(pe, Q0, m, p)), (1, summed(2)), (1, summed(3))), 3, 2)

        def act_linear(act):
            act.wait_ge(s.wt_ps, 1)
            act.activation(wqkvT[:, :], PS[:, 0, 0:3 * P], ACT.Copy).then_inc(s.wt, 1)

            def kept(m, par):
                within(act, s.g_hs, Q0, m + 1)
                hold(act, s.held)
                act.activation(X1[:, cols(m * BANK, BANK)], HSG[:, par, :], ACT.Copy).then_inc(s.c_cp, 1)

            def scaled(m, par):
                within(act, s.g_tb, Q0, m + 1)
                within(act, s.c_qkv, 0, m - 1)
                b = bass.ds(batch(m, 1), 1)
                hold(act, s.held)
                act.activation(HFG[:, par, :], PS[:, 6, :], ACT.Identity, bias=modc[:, 1, 0, b], scale=modc[:, 1, 1, b]).then_inc(s.g_h, 1)

            def centered(m, par):
                within(act, s.g_nb, 0, m + 1)
                within(act, s.g_tb, Q0, m)
                for i in range(4):
                    x = act.activation(HNG[:, i, :], PS[:, 5, i * P:(i + 1) * P], ACT.Identity, bias=nbg[:, i:i + 1], scale=rsg[:, i:i + 1])
                x.then_inc(s.g_x, 1)

            def exponentials(m, par):
                within(act, s.c_qkv, 0, m + 1)
                within(act, s.c_kv, 0, m * 2 - 2)
                within(act, s.c_kvp, 0, m * 2 - 2)
                within(act, s.c_sub, 0, m * 2 + 2)
                act.activation(VT[:, par, :, :], PS[:, 0:4, 2 * D:3 * D], ACT.Copy).then_inc(s.c_v, 1)
                act.activation(QKE[:, par, :, :], QKE[:, par, :, :], ACT.Exp).then_inc(s.c_e, 1)

            pipeline(act, GROUPS, GROUPS + 1, ((-1, kept), (1, exponentials), (0, centered), (0, scaled)), 3, 2)

        def dve_linear(dve):
            def input_group(m, par):
                within(dve, s.g_tp, Q0, m - 1)
                within(dve, s.c_cp, 0, m - 1)
                b = batch(m, 1)
                dve.scalar_tensor_tensor(HSG[:, par, :], XA[:, cols(gtok(m), BANK)], gcol[:, 0, 1, cols(b, 1)],
                                         X1[:, cols(m * BANK, BANK)], ALU.mult, ALU.add).then_inc(s.g_hs, 1)

            logits = PS[:, 0:4, 0:2 * D]

            def shifts(m, par):
                within(dve, s.g_r, Q0, m + 1)
                dve.scalar_tensor_tensor(nbg[:, :], mvg[:, :, 0], -1.0, rsg[:, :], ALU.mult, ALU.mult).then_inc(s.g_nb, 1)

            def maxima(m, par):
                within(dve, s.c_qkv, 0, m + 1)
                for part, x in zip((slice(0, H1), slice(H1, H1 + HD1)), by_softmax(logits)):
                    y = dve.tensor_reduce(MX[:, :, part], x, AX_X, ALU.max)
                y.then_inc(s.c_max, 1)
                within(dve, s.c_max, 0, m + 1)
                within(dve, s.c_kvp, 0, m * 2 - 2)
                within(dve, s.c_qt, 0, m * 4 - 4)
                for o, x, y in zip(by_softmax(QKE[:, par, :, :]), by_softmax(logits), spread(MX)):
                    dve.tensor_tensor(o, x, y, ALU.subtract).then_inc(s.c_sub, 1)

            def sums(m, par):
                within(dve, s.c_e, 0, m + 1)
                for part, x in zip((slice(0, H1), slice(H1, H1 + HD1)), by_softmax(QKE[:, par, :, :])):
                    y = dve.tensor_reduce(ZS[:, :, part], x, AX_X, ALU.add)
                y.then_inc(s.c_sum, 1)
                within(dve, s.c_sum, 0, m + 1)
                within(dve, s.c_qn, 0, m)
                dve.reciprocal(ZI, ZS).then_inc(s.c_rec, 1)

            def normalised_sum(m, i):
                within(dve, s.c_t0, 0, m * 4 + (i + 1))
                within(dve, s.c_qt, 0, m * 4 + (i - 3))
                dve.tensor_tensor(TT[:, i, :].rearrange("p (d e) -> p d e", e=HD1), KVs[:, i % 2, :].rearrange("p (d e) -> p d e", e=HD1),
                                  ZI[:, i, H1:].unsqueeze(2).to_broadcast([P, HD1, HD1]), ALU.mult).then_inc(s.c_t, 1)

            def products(m, par):
                within(dve, s.c_v, 0, m + 1)
                within(dve, s.c_t0, 0, m * 4)
                key_value(dve, par, 0, s.c_kv)
                key_value(dve, par, 1, s.c_kv)
                for i in range(4):
                    if i < 2:
                        within(dve, s.c_kv, 0, m * 2 + (i + 1))
                    else:
                        within(dve, s.c_kvp, 0, m * 2 + (i - 1))
                    within(dve, s.c_t, 0, m * 4 + (i - 1))
                    dve.tensor_reduce(KVs[:, i % 2, :], KV[:, i, :, :].rearrange("p h c -> p c h"), AX_X, ALU.add).then_inc(s.c_t0, 1)
                    if i > 0:
                        normalised_sum(m, i - 1)
                normalised_sum(m, 3)

            def residual(m, par):
                within(dve, s.c_o, 0, m * 4 + 4)
                within(dve, s.c_cp, 0, m + 1)
                c = cols(m * BANK, BANK)
                dve.scalar_tensor_tensor(X1[:, c], PS[:, 4, :], gcol[:, 1, 0, cols(batch(m, 1), 1)], X1[:, c], ALU.mult, ALU.add).then_inc(s.c_x3, 1)

            pipeline(dve, GROUPS, GROUPS + 2, ((1, maxima), (-1, input_group), (0, lambda m, p: dve_stats(dve, Q0, m, p)),
                                               (1, sums), (2, residual), (0, shifts), (1, products)), 3, 2)

        def pool_linear(pool):
            def products(m, par):
                within(pool, s.c_v, 0, m + 1)
                within(pool, s.c_e, 0, m + 1)
                within(pool, s.c_t0, 0, m * 4)
                key_value(pool, par, 2, s.c_kvp)
                key_value(pool, par, 3, s.c_kvp)
                within(pool, s.c_rec, 0, m + 1)
                q = by_softmax(QKE[:, par, :, :])[0]
                pool.tensor_tensor(q, q, spread(ZI)[0], ALU.mult).then_inc(s.c_qn, 1)
                within(pool, s.c_qn, 0, m + 1)
                for i in range(4):
                    within(pool, s.c_t, 0, m * 4 + (i + 1))
                    within(pool, s.c_o, 0, m * 4 + (i - 3))
                    pool.tensor_tensor(QT[:, i, :, :].rearrange("p d (h e) -> p d h e", e=HD1),
                                       QKE[:, par, i, 0:D].rearrange("p (h d) -> p d h", d=HD1).unsqueeze(3).to_broadcast([P, HD1, H1, HD1]),
                                       TT[:, i, :].rearrange("p (d e) -> p d e", e=HD1).unsqueeze(2).to_broadcast([P, HD1, H1, HD1]),
                                       ALU.mult).then_inc(s.c_qt, 1)

            pipeline(pool, GROUPS, GROUPS + 1, ((0, lambda m, p: pool_rstd(pool, Q0, m, p)), (1, products)), 3, 2)

        cut5 = Cut()
        GD, YD, XF, OB = cut5(2, 4, BANK), cut5(BANK), cut5(2, BANK), cut5(2, 4, P)
        Q1 = Q0 + GROUPS

        def pe_butterfly(pe):
            pe.wait_ge(s.c_x3, GROUPS)
            pe.wait_ge(s.bd_y, STAGES)
            for j in range(4):
                x = pe.transpose(PS[:, 0, j * P:(j + 1) * P], wdT[:, j * P:(j + 1) * P], ident[:, :])
            x.then_inc(s.wd_ps, 1)
            pe.wait_ge(s.bb_y, STAGES)
            pe.matmul(PS[:, 1, 0:HI], srow[0:LO, :], b_lo[0:LO, :], start=True, stop=True).then_inc(s.wd_ps, 1)
            pe.wait_ge(s.wd, 2)

            def up(m, par):
                within(pe, s.g_h, Q1, m + 1)
                for j in range(4):
                    within(pe, s.d_g, 0, m * 4 + (j - 3))
                    pe.matmul(PS[:, j, :], wu[:, j * P:(j + 1) * P], HFG[:, par, :], start=True, stop=True).then_inc(s.d_up, 1)

            def down(m, par):
                within(pe, s.d_g, 0, m * 4 + 4)
                within(pe, s.d_y, 0, m)
                for j in range(4):
                    x = pe.matmul(PS[:, 4, :], wd[:, j, :], GD[:, par, j, :], start=(j == 0), stop=(j == 3))
                x.then_inc(s.d_dn, 1)

            def turn_out(m, par):
                within(pe, s.d_x4, 0, m + 1)
                within(pe, s.d_o, 0, m)
                for i in range(4):
                    x = pe.transpose(PS[:, 7, i * P:(i + 1) * P], XF[:, par, i * P:(i + 1) * P], ident[:, :])
                x.then_inc(s.d_ot, 1)

            pipeline(pe, GROUPS, GROUPS + 3, ((3, turn_out), (1, up), (2, down), (0, lambda m, p: pe_turn_back(pe, Q1, m, p)),
                                              (-1, lambda m, p: pe_turn(pe, Q1, m, p))), 4, 1)

        def act_butterfly(act):
            act.wait_ge(s.wd_ps, 1)
            act.activation(wd[:, :, :], PS[:, 0, :].rearrange("p (j d) -> p j d", j=4), ACT.Copy).then_inc(s.wd, 1)

            def gelus(m, par):
                for j in range(4):
                    within(act, s.d_up, 0, m * 4 + j + 1)
                    within(act, s.d_dn, 0, m - 1)
                    act.activation(GD[:, par, j, :], PS[:, j, :], ACT.Gelu, bias=bcol[:, j:j + 1]).then_inc(s.d_g, 1)

            def scaled(m, par):
                within(act, s.g_tb, Q1, m + 1)
                within(act, s.d_up, 0, (m - 1) * 4)
                b = bass.ds(batch(m, 1), 1)
                hold(act, s.held)
                act.activation(HFG[:, par, :], PS[:, 6, :], ACT.Identity, bias=modc[:, 1, 3, b], scale=modc[:, 1, 4, b]).then_inc(s.g_h, 1)

            def outputs(m, par):
                within(act, s.d_ot, 0, m + 1)
                within(act, stored[par], 0, (m >> 1) * 16)
                act.activation(OB[:, par, :, :], PS[:, 7, :].rearrange("p (i d) -> p i d", i=4), ACT.Copy).then_inc(s.d_o, 1)

            pipeline(act, GROUPS, GROUPS + 3, ((3, outputs), (1, gelus), (0, scaled)), 5, 1)

        def dve_butterfly(dve):
            dve.wait_ge(s.l1_cols, 16 * 3)
            dve.wait_ge(s.wd_ps, 2)
            dve.tensor_tensor(b_sel[:, :, :], PS[:, 1, 0:HI].rearrange("p (j g) -> p j g", j=4), chan[:, :].unsqueeze(1).to_broadcast([P, 4, CG]),
                              ALU.mult).then_inc(s.bb_sel, 1)
            dve.wait_ge(s.bb_sel, 2)
            dve.tensor_reduce(bcol[:, 0:4], b_sel[:, :, :], AX_X, ALU.add).then_inc(s.bb_sel, 1)
            dve.wait_ge(s.bb_sel, 3)
            dve.tensor_tensor(bcol[:, 0:4], bcol[:, 0:4], bcols[:, 0:4], ALU.add).then_inc(s.wd, 1)
            dve.tensor_tensor(bcol[:, 4:5], bcols[:, 4:5], bcols[:, 5:6], ALU.add).then_inc(s.bcol, 1)
            dve.wait_ge(s.bcol, 1)

            def gated(m, par):
                within(dve, s.d_dn, 0, m + 1)
                within(dve, s.d_x4, 0, m)
                dve.tensor_scalar(YD, PS[:, 4, :], bcol[:, 4:5], gcol[:, 1, 1, cols(batch(m, 1), 1)], ALU.add, ALU.mult).then_inc(s.d_y, 1)
                within(dve, s.d_y, 0, m + 1)
                within(dve, s.d_ot, 0, m - 1)
                dve.tensor_tensor(XF[:, par, :], YD, X1[:, cols(m * BANK, BANK)], ALU.add).then_inc(s.d_x4, 1)

            pipeline(dve, GROUPS, GROUPS + 2, ((0, lambda m, p: dve_stats(dve, Q1, m, p)), (0, lambda m, p: dve_center(dve, Q1, m, p)), (2, gated)), 4, 2)

        def pool_butterfly(pool):
            def taken(m, par):
                within(pool, s.g_tp, Q1, m - 1)
                pool.wait_ge(s.c_x3, GROUPS)
                hold(pool, s.held)
                pool.tensor_copy(HSG[:, par, :], X1[:, cols(m * BANK, BANK)]).then_inc(s.g_hs, 1)

            pipeline(pool, GROUPS, GROUPS + 2, ((0, lambda m, p: pool_rstd(pool, Q1, m, p)), (-1, taken)), 2, 2)

        def pool_compose(pool):
            pool.wait_ge(s.cweights, 16)
            for n in range(STAGES):
                pool.wait_ge(bw[n % 2], 16 * (n // 2 + 1))
                butterfly_stage(pool, n, wu, bwr[:, n % 2, :], cmp, False, 1 << n, s.bu_t, s.bu_y)
            pool.wait_ge(s.wc, 1)
            for n in range(STAGES):
                m = STAGES + n
                pool.wait_ge(bw[m % 2], 16 * (m // 2 + 1))
                butterfly_stage(pool, n, wdT, bwr[:, m % 2, :], cmp, True, 1 << (STAGES - 1 - n), s.bd_t, s.bd_y)

        @block.sync
        def _(sp):
            for h, sx in enumerate((s.x0, s.x1)):
                sp.dma_start(XP[:, h, :, :], x_rows[P * h:P * h + P, :].rearrange("p (i d) -> p i d", i=CH)).then_inc(sx, 16)
            for n, pre in enumerate(("L0", "L1")):
                sp.dma_start(cT[:, n, :], a[pre + "_c"].rearrange("b k -> k b")).then_inc(s.params, 16)
                sp.dma_start(wmod[:, n, :], a[pre + "_wmod"]).then_inc(s.params, 16)
            for t, name in ((ident, "ident"), (srow, "srow"), (chan, "chan"), (powers, "powers"), (signs, "signs"), (anti, "anti")):
                sp.dma_start(t[:, :], a[name]).then_inc(s.consts, 16)
            sp.dma_start(A_row[0:S, :], a["L0_attn_A_log"]).then_inc(s.params, 16)
            sp.dma_start(B_row[0:S, :], a["L0_attn_B"]).then_inc(s.params, 16)
            sp.dma_start(C_col[:, :], a["L0_attn_C"]).then_inc(s.params, 16)
            sp.dma_start(D_row[0:1, :], a["L0_attn_D"].rearrange("(o d) -> o d", o=1)).then_inc(s.params, 16)
            sp.dma_start(shift[:, :], a["shift"]).then_inc(s.consts, 16)
            sp.dma_start(wu[:, :], a["L1_ffn_W_exp"]).then_inc(s.cweights, 16)
            sp.dma_start(wcon[:, :, :], a["L1_ffn_W_con"].rearrange("(j p) d -> p j d", p=P)).then_inc(s.wconl, 16)
            sp.dma_start(ropec[:, :, :, :], a["rope"].rearrange("p t (f d) -> p t f d", f=4)).then_inc(s.tables, 16)
            sp.dma_start(maskf[:, :, :], a["masks"]).then_inc(s.tables, 16)
            up = a["L1_ffn_up_weights"]
            sp.dma_start(b_hi[0:HI, :], a["L1_ffn_b_exp"].rearrange("(p n) -> p n", n=LO)).then_inc(s.bias_w, 16)
            for k in range(LO_BITS):
                sp.dma_start(w_hi[0:HI, k, :], up[k, :, :, :].rearrange("(p n) o i -> p (n o i)", p=HI)).then_inc(s.bias_w, 16)
            for k in range(LO_BITS, STAGES):
                sp.dma_start(w_lo[0:LO, k - LO_BITS, :, :], up[k, :, :, :].rearrange("(g l) o i -> l g (o i)", l=LO)).then_inc(s.bias_w, 16)
            sp.dma_start(bcols[:, 0:4], a["L1_ffn_up_bias"].rearrange("(j p) -> p j", p=P)).then_inc(s.l1_cols, 16)
            for j, name in enumerate(("L1_ffn_b_con", "L1_ffn_down_bias")):
                sp.dma_start(bcols[:, 4 + j:5 + j], a[name].rearrange("(p o) -> p o", o=1)).then_inc(s.l1_cols, 16)
            for j, name in enumerate(("L1_attn_W_Q", "L1_attn_W_K", "L1_attn_W_V")):
                sp.dma_start(wq1[:, j, :], a[name]).then_inc(s.l1_weights, 16)
            stage_weights(sp)
            for l in range(DEPTH):
                wait(sp, s.att_res, TILES * l)
                sp.dma_start(wqkv[:, :], a["L0_ffn_wqkv"][l, :, :]).then_inc(s.att_weights, 16)
                sp.dma_start(wo[:, :, :], a["L0_ffn_wo"][l, :, :].rearrange("(t p) n -> p t n", p=P)).then_inc(s.att_weights, 16)
                wait(sp, s.rope_s, l)
                for j, name in enumerate(("L0_ffn_q_scale", "L0_ffn_k_scale")):
                    sp.dma_start(qks[:, j, :], a[name][l:l + 1, :].to_broadcast([P, DH])).then_inc(s.att_weights, 16)
                wait(sp, s.m_res, GROUPS * l)
                sp.dma_start(w1[:, :], a["L0_ffn_w1"][l, :, :]).then_inc(s.ffn_weights, 16)
                sp.dma_start(w2[:, 0:2, :], a["L0_ffn_w2"][l, 0:2 * P, :].rearrange("(t p) n -> p t n", p=P)).then_inc(s.ffn_weights, 16)
                sp.dma_start(w2[0:HID - 2 * P, 2, :], a["L0_ffn_w2"][l, 2 * P:HID, :]).then_inc(s.ffn_weights, 16)
                for j, name in enumerate(("L0_ffn_ln_g", "L0_ffn_ln_b", "L0_ffn_b2")):
                    sp.dma_start(lgc[:, j:j + 1], a[name][l:l + 1, :].rearrange("o d -> d o")).then_inc(s.ffn_weights, 16)
                for half in range(2):
                    for t, (j, k) in enumerate(HT):
                        col = half * HID + j
                        sp.dma_start(b1c[0:k, half, t:t + 1], a["L0_ffn_b1"][l:l + 1, col:col + k].rearrange("o d -> d o")).then_inc(s.ffn_weights, 16)

            with sp.Fori(0, GROUPS // 2) as m:
                for par in range(2):
                    sp.wait_ge(s.d_o, m * 2 + (par + 1))
                    sp.dma_start(out_rows[bass.ds(m * 8 + par * 4, 4), :, :].rearrange("t p d -> p t d"), OB[:, par, :, :]).then_inc(stored[par], 16)
            for par in range(2):
                sp.wait_ge(stored[par], 16 * GROUPS // 2)


        @block.tensor
        def _(pe):
            pe_state_space(pe)
            pe_start(pe)
            attention_layers(pe, pe_attention, pe_ffn)
            pe_linear(pe)
            pe_butterfly(pe)

        @block.scalar
        def _(act):
            act_state_space(act)
            attention_layers(act, act_attention, act_ffn)
            act_linear(act)
            act_butterfly(act)

        @block.vector
        def _(dve):
            dve_state_space(dve)
            dve_bias(dve)
            attention_layers(dve, dve_attention, dve_ffn, each=dve_rope)
            dve_linear(dve)
            dve_butterfly(dve)

        @block.gpsimd
        def _(pool):
            pool_setup(pool)
            pool_start(pool)
            attention_layers(pool, pool_attention, pool_ffn)
            pool_linear(pool)
            pool_butterfly(pool)


def kernel(**inputs):
    import numpy as _np
    import concourse.bacc as _bacc
    from concourse import mybir as _mybir
    from concourse.bass_utils import run_bass_kernel_spmd as _run

    nc = _bacc.Bacc("TRN2", target_bir_lowering=False, num_devices=1)
    arrays, aps = {}, {}
    for name, v in [*inputs.items(), *shape_constants().items()]:
        v = _np.ascontiguousarray(v)
        arrays[f"in_{name}"] = v
        aps[name] = nc.dram_tensor(f"in_{name}", v.shape, _mybir.dt.from_np(v.dtype), kind="ExternalInput").ap()
    out = nc.dram_tensor("out_x", (B, N, D), F32, kind="ExternalOutput").ap()
    build(nc, aps, out)
    r = _run(nc, [arrays], core_ids=[0])
    return r.results[0]["out_x"]
```
